# Optimizing a Trainium2 kernel written in Bass

```python
import numpy as np
import jax
import jax.numpy as jnp

def _softmax(x, axis=-1):
    return jax.nn.softmax(x, axis=axis)

def _gelu(x):
    return jax.nn.gelu(x, approximate=True)

def _silu(x):
    return jax.nn.silu(x)

def _sigmoid(x):
    return jax.nn.sigmoid(x)

def _layernorm(x, axis=-1, eps=1e-05):
    m = jnp.mean(x, axis=axis, keepdims=True)
    v = jnp.var(x, axis=axis, keepdims=True)
    return (x - m) / jnp.sqrt(v + eps)

def _scatter_add(tgt, idx, src, axis=0):
    return tgt.at[idx].add(src)

def _segment_sum(src, seg, n):
    return jax.ops.segment_sum(src, seg, n)
kernel_name = 'mk_perceiver_d1_seqx_r4_7771d5'

def setup_inputs(seed: int=0):
    np.random.seed(seed)
    _w = jnp.asarray

    def _rec_inputs():
        import jax
        import jax.numpy as jnp
        _rk = jax.random.key(seed)
        x = -0.000125 + 0.9999 * jax.random.normal(jax.random.fold_in(_rk, 1), (64, 64, 256), jnp.float32)
        _lenS = 64 - jax.random.randint(jax.random.fold_in(_rk, 7), (64,), 0, max(1, 64 // 4) + 1, jnp.int32)
        _lenS2 = 256 - jax.random.randint(jax.random.fold_in(_rk, 8), (64,), 0, max(1, 256 // 4) + 1, jnp.int32)
        _ctx_768P = jax.random.normal(jax.random.fold_in(_rk, 11), (64, 16, 192), jnp.float32)
        _ctx_768c = jax.random.dirichlet(jax.random.fold_in(_rk, 511), 0.3 * jnp.ones((16,), jnp.float32), (64, 256))
        _ctx_768t = jnp.einsum('bsk,bkd->bsd', _ctx_768c, _ctx_768P)
        _ctx_768t = _ctx_768t * jax.lax.rsqrt(jnp.mean(jnp.square(_ctx_768t)) + 1e-12) * 0.953939
        ctx_768 = 0.00272024 + 0.999456 * (_ctx_768t + 0.3 * jax.random.normal(jax.random.fold_in(_rk, 611), (64, 256, 192), jnp.float32))
        return (x, ctx_768)
    x, ctx_768 = _rec_inputs()

    def _L0_xattn_setup():
        import jax, jax.numpy as jnp
        import numpy as np
        HEADS = 16
        DIM_HEAD = 64
        SCALE = DIM_HEAD ** (-0.5)
        QUERY_DIM = 256
        CONTEXT_DIM = 192
        INNER_DIM = HEADS * DIM_HEAD
        key = jax.random.key(seed)
        ks = jax.random.split(key, 7)
        B, Nq, Nk = (8, 1024, 77)
        x = jax.random.normal(ks[0], (B, Nq, QUERY_DIM), dtype=jnp.float32)
        context = jax.random.normal(ks[1], (B, Nk, CONTEXT_DIM), dtype=jnp.float32)
        Wq = jax.random.normal(ks[2], (QUERY_DIM, INNER_DIM), dtype=jnp.float32) * QUERY_DIM ** (-0.5)
        Wk = jax.random.normal(ks[3], (CONTEXT_DIM, INNER_DIM), dtype=jnp.float32) * CONTEXT_DIM ** (-0.5)
        Wv = jax.random.normal(ks[4], (CONTEXT_DIM, INNER_DIM), dtype=jnp.float32) * CONTEXT_DIM ** (-0.5)
        Wo = jax.random.normal(ks[5], (INNER_DIM, QUERY_DIM), dtype=jnp.float32) * INNER_DIM ** (-0.5)
        bo = jnp.zeros((QUERY_DIM,), dtype=jnp.float32)
        return {'x': x, 'context': context, 'Wq': Wq, 'Wk': Wk, 'Wv': Wv, 'Wo': Wo, 'bo': bo}
    _L0_xattn_all = _L0_xattn_setup()
    _L0_xattn_in = {k: v for k, v in _L0_xattn_all.items() if k in ('Wq', 'Wk', 'Wv', 'Wo', 'bo')}
    del _L0_xattn_all

    def _L0_attn_setup():
        import jax, jax.numpy as jnp
        import numpy as np
        N_HEADS = 16
        HEAD_DIM = 64
        HIDDEN = 256
        key = jax.random.key(seed)
        kx, kq, kk, kv, ko = jax.random.split(key, 5)
        B, S = (1, 1024)
        lim = float(np.sqrt(6.0 / (HIDDEN + N_HEADS * HEAD_DIM)))
        x = jax.random.normal(kx, (B, S, HIDDEN), dtype=jnp.float32)
        wq = jax.random.uniform(kq, (N_HEADS * HEAD_DIM, HIDDEN), jnp.float32, -lim, lim)
        wk = jax.random.uniform(kk, (N_HEADS * HEAD_DIM, HIDDEN), jnp.float32, -lim, lim)
        wv = jax.random.uniform(kv, (N_HEADS * HEAD_DIM, HIDDEN), jnp.float32, -lim, lim)
        wo = jax.random.uniform(ko, (HIDDEN, N_HEADS * HEAD_DIM), jnp.float32, -lim, lim)
        return {'x': x, 'wq': wq, 'wk': wk, 'wv': wv, 'wo': wo}
    _L0_attn_all = _L0_attn_setup()
    _L0_attn_in = {k: v for k, v in _L0_attn_all.items() if k in ('wq', 'wk', 'wv', 'wo')}
    del _L0_attn_all

    def _L0_ffn_setup():
        import jax, jax.numpy as jnp
        import numpy as np
        TOP_K = 2
        key = jax.random.key(seed)
        k1, k2, k3, k4, k5 = jax.random.split(key, 5)
        B, S, D, F, E = (2, 256, 256, 512, 8)
        return {'x': jax.random.normal(k1, (B, S, D), dtype=jnp.float32), 'router_kernel_DE': jax.random.normal(k2, (D, E), dtype=jnp.float32) * 0.02, 'kernel_gating_EDF': jax.random.normal(k3, (E, D, F), dtype=jnp.float32) * 0.02, 'kernel_up_EDF': jax.random.normal(k4, (E, D, F), dtype=jnp.float32) * 0.02, 'kernel_down_EFD': jax.random.normal(k5, (E, F, D), dtype=jnp.float32) * 0.02}
    _L0_ffn_all = _L0_ffn_setup()
    _L0_ffn_in = {k: v for k, v in _L0_ffn_all.items() if k in ('router_kernel_DE', 'kernel_gating_EDF', 'kernel_up_EDF', 'kernel_down_EFD')}
    del _L0_ffn_all
    return {'x': x, 'ctx_768': ctx_768, 'L0_xattn_Wq': _L0_xattn_in['Wq'], 'L0_xattn_Wk': _L0_xattn_in['Wk'], 'L0_xattn_Wv': _L0_xattn_in['Wv'], 'L0_xattn_Wo': _L0_xattn_in['Wo'], 'L0_xattn_bo': _L0_xattn_in['bo'], 'L0_attn_wq': _L0_attn_in['wq'], 'L0_attn_wk': _L0_attn_in['wk'], 'L0_attn_wv': _L0_attn_in['wv'], 'L0_attn_wo': _L0_attn_in['wo'], 'L0_ffn_router_kernel_DE': _L0_ffn_in['router_kernel_DE'], 'L0_ffn_kernel_gating_EDF': _L0_ffn_in['kernel_gating_EDF'], 'L0_ffn_kernel_up_EDF': _L0_ffn_in['kernel_up_EDF'], 'L0_ffn_kernel_down_EFD': _L0_ffn_in['kernel_down_EFD']}

def reference(x, ctx_768, L0_xattn_Wq, L0_xattn_Wk, L0_xattn_Wv, L0_xattn_Wo, L0_xattn_bo, L0_attn_wq, L0_attn_wk, L0_attn_wv, L0_attn_wo, L0_ffn_router_kernel_DE, L0_ffn_kernel_gating_EDF, L0_ffn_kernel_up_EDF, L0_ffn_kernel_down_EFD):
    import jax
    import jax.numpy as jnp

    def _L0_xattn_ref(x, context, Wq, Wk, Wv, Wo, bo):
        import jax, jax.numpy as jnp
        import numpy as np
        HEADS = 16
        DIM_HEAD = 64
        SCALE = DIM_HEAD ** (-0.5)
        QUERY_DIM = 256
        CONTEXT_DIM = 192
        INNER_DIM = HEADS * DIM_HEAD
        B, Nq, _ = x.shape
        Nk = context.shape[1]
        q = x @ Wq
        k = context @ Wk
        v = context @ Wv
        q = q.reshape(B, Nq, HEADS, DIM_HEAD).transpose(0, 2, 1, 3)
        k = k.reshape(B, Nk, HEADS, DIM_HEAD).transpose(0, 2, 1, 3)
        v = v.reshape(B, Nk, HEADS, DIM_HEAD).transpose(0, 2, 1, 3)
        sim = jnp.einsum('bhid,bhjd->bhij', q, k) * SCALE
        attn = jax.nn.softmax(sim, axis=-1)
        out = jnp.einsum('bhij,bhjd->bhid', attn, v)
        out = out.transpose(0, 2, 1, 3).reshape(B, Nq, INNER_DIM)
        return out @ Wo + bo

    def _L0_attn_ref(x, wq, wk, wv, wo):
        import jax, jax.numpy as jnp
        import numpy as np
        N_HEADS = 16
        HEAD_DIM = 64
        HIDDEN = 256
        B, S, _ = x.shape
        scale = HEAD_DIM ** (-0.5)

        def proj(w):
            return jnp.einsum('bsh,eh->bse', x, w).reshape(B, S, N_HEADS, HEAD_DIM).transpose(0, 2, 1, 3)
        q, k, v = (proj(wq), proj(wk), proj(wv))
        scores = jnp.einsum('bhqd,bhkd->bhqk', q, k) * scale
        causal = jnp.tril(jnp.ones((S, S), dtype=bool))
        scores = jnp.where(causal, scores, -jnp.inf)
        probs = jax.nn.softmax(scores, axis=-1)
        out = jnp.einsum('bhqk,bhkd->bhqd', probs, v)
        out = out.transpose(0, 2, 1, 3).reshape(B, S, N_HEADS * HEAD_DIM)
        return jnp.einsum('bse,he->bsh', out, wo)

    def _L0_ffn_ref(x, router_kernel_DE, kernel_gating_EDF, kernel_up_EDF, kernel_down_EFD):
        import jax, jax.numpy as jnp
        import numpy as np
        TOP_K = 2
        E = router_kernel_DE.shape[-1]
        x = x.astype(jnp.float32)
        logits_BSE = jnp.einsum('BSD,DE->BSE', x, router_kernel_DE)
        probs_BSE = jax.nn.softmax(logits_BSE.astype(jnp.float32), axis=-1)
        weights_BSK, indices_BSK = jax.lax.top_k(probs_BSE, TOP_K)
        norm_weights_BSK = jax.nn.softmax(weights_BSK, axis=-1)
        one_hot_BSKE = jax.nn.one_hot(indices_BSK, num_classes=E, dtype=x.dtype)
        full_weights_BSE = jnp.sum(one_hot_BSKE * norm_weights_BSK[..., None], axis=2)
        gating_BSEF = jnp.einsum('BSD,EDF->BSEF', x, kernel_gating_EDF)
        act_BSEF = jax.nn.silu(gating_BSEF)
        up_BSEF = jnp.einsum('BSD,EDF->BSEF', x, kernel_up_EDF)
        fuse_BSEF = act_BSEF * up_BSEF
        down_BSED = jnp.einsum('BSEF,EFD->BSED', fuse_BSEF, kernel_down_EFD)
        out_BSD = jnp.einsum('BSED,BSE->BSD', down_BSED, full_weights_BSE)
        return out_BSD.astype(jnp.float32)
    x = x + _L0_xattn_ref(_layernorm(x, axis=-1), ctx_768, L0_xattn_Wq, L0_xattn_Wk, L0_xattn_Wv, L0_xattn_Wo, L0_xattn_bo)
    x = x + _L0_attn_ref(_layernorm(x, axis=-1), L0_attn_wq, L0_attn_wk, L0_attn_wv, L0_attn_wo)
    x = x + _L0_ffn_ref(_layernorm(x, axis=-1), L0_ffn_router_kernel_DE, L0_ffn_kernel_gating_EDF, L0_ffn_kernel_up_EDF, L0_ffn_kernel_down_EFD)
    return x

_drawn_inputs = setup_inputs


def setup_inputs(seed=0):
    import zlib

    import numpy as np

    out = dict(_drawn_inputs(seed))
    spreads = {'L0_xattn_bo': (0.0, 0.1)}
    factors = {'L0_ffn_router_kernel_DE': 4.71,
     'L0_ffn_kernel_gating_EDF': 4.11,
     'L0_ffn_kernel_up_EDF': 4.085,
     'L0_ffn_kernel_down_EFD': 4.076}
    for name, (base, spread) in spreads.items():
        noise = np.random.default_rng([zlib.crc32(name.encode()), seed]).standard_normal(out[name].shape)
        drawn = base * np.exp(spread * noise) if base else spread * noise
        out[name] = jnp.asarray(drawn.astype(out[name].dtype))
    for name, factor in factors.items():
        out[name] = (out[name] * factor).astype(out[name].dtype)
    return out
```

```python
from contextlib import ExitStack

import concourse.bass as bass
from concourse import mybir

ALU = mybir.AluOpType
ACT = mybir.ActivationFunctionType
AX_X = mybir.AxisListType.X
F32 = mybir.dt.float32
F32R = mybir.dt.float32r

P = 128
HEAD = 64
EPS = 1e-5
MASKED = -1e30
DMA = 16


def wait(eng, sem, value):
    if isinstance(value, int) and value <= 0:
        return
    eng.wait_ge(sem, value)


def f32(ap):
    return ap.bitcast(F32)


def split_hi_act(nc, hi, src, scale=None):
    if scale is None:
        return nc.scalar.copy(hi, src)
    return nc.scalar.mul(hi, src, scale)


def round_pool(nc, hi, src, zero):
    return nc.gpsimd.tensor_tensor(hi, src, zero[:].to_broadcast(list(src.shape)), ALU.add)


def split_lo_dve(nc, lo, src, hi, scale=None):
    if scale is None:
        return nc.vector.tensor_tensor(lo, src, f32(hi), ALU.subtract)
    return nc.vector.scalar_tensor_tensor(out=lo, in0=src, scalar=scale, in1=f32(hi),
                                          op0=ALU.mult, op1=ALU.subtract)


def three_pass(pe, out, pairs, skip=False):
    for i, (lhs, rhs) in enumerate(pairs):
        mm = pe.matmul(out, lhs, rhs, start=(i == 0), stop=(i == len(pairs) - 1))
    return mm


def hi_lo(a_hi, a_lo, b_hi, b_lo):
    return [(a_hi, b_hi), (a_lo, b_hi), (a_hi, b_lo)]


def layer_kernel(nc, x, ctx_t, wq, wk, wv, wo, bo, sq, sk, sv, so, router, w_gate, w_up, w_down, out):
    NTOK, D = x.shape
    TILES = NTOK // P
    DC = D // P
    _, C, TJ = ctx_t.shape
    J = TJ // 2
    REM = C - P
    E = wq.shape[1]
    PAIRS = E // P
    GROUPS = TILES // 2
    STEPS = TILES * PAIRS
    EXPERTS, _, F = w_gate.shape
    FC = F // P
    HALF = 512
    SCALE = HEAD ** -0.5
    assert REM == HEAD and DC == 2 and PAIRS == 8 and HALF == 2 * J and E == 2 * HALF

    with ExitStack() as root:
        def sem(name):
            return root.enter_context(nc.semaphore(name))

        def sbuf(stack, name, shape, dt=F32):
            return stack.enter_context(nc.sbuf_tensor(name, shape, dt))

        def psum(stack, name, shape=(P, HALF)):
            return stack.enter_context(nc.psum_tensor(name, list(shape), F32))

        x_sb = sbuf(root, "x_sb", [P, TILES, D])
        ident = sbuf(root, "ident", [P, P])
        mask = sbuf(root, "mask", [P, 4, P])
        neg_half = sbuf(root, "neg_half", [P, 2])
        zero = sbuf(root, "zero", [P, 1])

        def load_weights(phase, jobs):
            with ExitStack() as st:
                stage = sbuf(st, f"stage_{phase}", [P, 2, 2048])
                loaded = [sem(f"w_loaded_{phase}_{i}") for i in range(2)]
                his = sem(f"w_hi_{phase}")
                los = sem(f"w_lo_{phase}")
                block = st.enter_context(nc.Block())

                @block.sync
                def _(sp):
                    for n, (dmas, cols, hi, lo) in enumerate(jobs):
                        wait(sp, los, n - 1)
                        for (r0, r1, c0, c1, src) in dmas:
                            dst = stage[r0:r1, n % 2, c0:c1]
                            if len(src.shape) == 3:
                                dst = dst.rearrange("p (c n) -> p c n", c=src.shape[1])
                            sp.dma_start(dst, src).then_inc(loaded[n % 2], DMA)

                def arrived(n):
                    return DMA * sum(len(jobs[m][0]) for m in range(n % 2, n + 1, 2))

                @block.scalar
                def _(act):
                    for n, (dmas, cols, hi, lo) in enumerate(jobs):
                        act.wait_ge(loaded[n % 2], arrived(n))
                        split_hi_act(nc, hi, stage[:, n % 2, 0:cols]).then_inc(his, 1)

                @block.vector
                def _(dve):
                    for n, (dmas, cols, hi, lo) in enumerate(jobs):
                        dve.wait_ge(his, n + 1)
                        split_lo_dve(nc, lo, stage[:, n % 2, 0:cols], hi).then_inc(los, 1)

        def pair_of(stack, name, cols):
            return (sbuf(stack, name + "_hi", [P, cols], F32R), sbuf(stack, name + "_lo", [P, cols], F32R))

        def ln_buffers(stack, phase):
            return dict(
                stats=sbuf(stack, f"ln_stats_{phase}", [P, 2, 6]),
                mv=sbuf(stack, f"ln_mv_{phase}", [P, 2, 2]),
                veps=sbuf(stack, f"ln_veps_{phase}", [P, 2]),
                rstd=sbuf(stack, f"ln_rstd_{phase}", [P, 2]),
                xn=sbuf(stack, f"ln_xn_{phase}", [P, 2, D]),
                gate=sbuf(stack, f"ln_gate_{phase}", [P, 1]), s_gate=sem(f"ln_gate_done_{phase}"),
                s_stats=sem(f"ln_stats_done_{phase}"), s_mv=sem(f"ln_mv_done_{phase}"),
                s_veps=sem(f"ln_veps_done_{phase}"), s_rstd=sem(f"ln_rstd_done_{phase}"),
                s_xn=sem(f"ln_xn_done_{phase}"))

        def ln_stats(dve, ln, g):
            wait(dve, ln["s_xn"], 2 * g)
            for u in range(2):
                nc.vector.bn_stats(ln["stats"][:, u, :], x_sb[:, 2 * g + u, :]).then_inc(ln["s_stats"], 1)
            wait(dve, ln["s_gate"], g)
            dve.wait_ge(ln["s_stats"], 2 * g + 2)
            nc.vector.memset(ln["gate"][:], 0.0).then_inc(ln["s_gate"], 1)
            for u in range(2):
                nc.vector.bn_aggr(ln["mv"][:, u, :], ln["stats"][:, u, :]).then_inc(ln["s_mv"], 1)
            dve.wait_ge(ln["s_mv"], 2 * g + 2)
            nc.vector.tensor_scalar(ln["veps"][:], ln["mv"][:, :, 1], EPS, None, ALU.add).then_inc(ln["s_veps"], 1)

        def ln_rstd(pool, ln, g):
            pool.wait_ge(ln["s_veps"], g + 1)
            nc.gpsimd.tensor_tensor(ln["rstd"][:], ln["veps"][:], neg_half[:], ALU.pow).then_inc(ln["s_rstd"], 1)

        def ln_apply(dve, ln, g):
            dve.wait_ge(ln["s_rstd"], g + 1)
            for u in range(2):
                nc.vector.tensor_scalar(ln["xn"][:, u, :], x_sb[:, 2 * g + u, :], ln["mv"][:, u, 0:1],
                                        ln["rstd"][:, u:u + 1], ALU.subtract, ALU.mult).then_inc(ln["s_xn"], 1)

        s_x = sem("x_loaded")
        s_const = sem("const_ready")
        with nc.Block() as block:
            @block.sync
            def _(sp):
                sp.dma_start(x_sb[:], x.rearrange("(t p) d -> p t d", p=P)).then_inc(s_x, DMA)
                sp.wait_ge(s_x, DMA)

            @block.gpsimd
            def _(pool):
                nc.gpsimd.memset(ident[:], 0.0).then_inc(s_const, 1)
                nc.gpsimd.memset(mask[:], 0.0).then_inc(s_const, 1)
                nc.gpsimd.memset(neg_half[:], -0.5).then_inc(s_const, 1)
                nc.gpsimd.memset(zero[:], 0.0).then_inc(s_const, 1)
                pool.wait_ge(s_const, 4)
                nc.gpsimd.affine_select(out=ident[:], in_=ident[:], compare_op=ALU.not_equal, fill=1.0, base=0,
                                        pattern=[[-1, P]], channel_multiplier=1).then_inc(s_const, 1)
                nc.gpsimd.affine_select(out=mask[:], in_=mask[:], compare_op=ALU.is_ge, fill=MASKED, base=0,
                                        pattern=[[0, 4], [-1, P]], channel_multiplier=1).then_inc(s_const, 1)
                pool.wait_ge(s_const, 6)
                nc.gpsimd.memset(mask[HEAD:P, :, 0:HEAD], MASKED).then_inc(s_const, 1)
                pool.wait_ge(s_const, 7)

        with ExitStack() as ph:
            bo_b = sbuf(ph, "bo_b", [P, D])
            wq_hi, wq_lo = pair_of(ph, "wq", DC * E)
            wk_hi, wk_lo = pair_of(ph, "wk", 2 * E)
            wv_hi, wv_lo = pair_of(ph, "wv", 2 * E)
            wo_hi, wo_lo = pair_of(ph, "wo", PAIRS * D)

            def rows_192(w):
                return [(0, P, 0, E, w[0:P, :]), (0, REM, E, 2 * E, w[P:C, :]), (REM, P, E, 2 * E, w[P:C, :])]

            load_weights("x", [
                ([(0, P, 0, DC * E, wq.rearrange("(c p) n -> p c n", p=P))], DC * E, wq_hi[:], wq_lo[:]),
                (rows_192(wk), 2 * E, wk_hi[:], wk_lo[:]),
                (rows_192(wv), 2 * E, wv_hi[:], wv_lo[:]),
                ([(0, P, 0, PAIRS * D, wo.rearrange("(c p) n -> p c n", p=P))], PAIRS * D, wo_hi[:], wo_lo[:]),
            ])

            ctx_raw = sbuf(ph, "ctx_raw", [P, 2, 2, HALF])
            cx_hi = sbuf(ph, "cx_hi", [P, 2, HALF], F32R)
            cx_lo = sbuf(ph, "cx_lo", [P, 2, HALF], F32R)
            cx_rem = sbuf(ph, "cx_rem", [P, 2, HALF], F32R)
            qbd_hi = sbuf(ph, "qbd_hi", [P, PAIRS, 4, P], F32R)
            qbd_lo = sbuf(ph, "qbd_lo", [P, PAIRS, 4, P], F32R)
            kt_hi = sbuf(ph, "kt_hi", [P, 2, HALF], F32R)
            kt_lo = sbuf(ph, "kt_lo", [P, 2, HALF], F32R)
            v_sb = sbuf(ph, "v_sb", [P, 4, E])
            p_sb = sbuf(ph, "p_sb", [P, 4, HALF])
            pt_sb = sbuf(ph, "pt_sb", [P, 2, HALF])
            ot_hi = sbuf(ph, "ot_hi", [P, PAIRS, P], F32R)
            ot_lo = sbuf(ph, "ot_lo", [P, PAIRS, P], F32R)
            xt_hi = sbuf(ph, "xt_hi", [P, DC, 2 * P], F32R)
            xt_lo = sbuf(ph, "xt_lo", [P, DC, 2 * P], F32R)
            nmax = sbuf(ph, "nmax", [P, 4, 2])
            rsum = sbuf(ph, "rsum", [P, 4, 2])
            rinv = sbuf(ph, "rinv", [P, 4, 2])
            ln = ln_buffers(ph, "x")

            k_ps = psum(ph, "k_ps")
            v_ps = psum(ph, "v_ps")
            s_ps = [psum(ph, f"s_ps{i}") for i in range(2)]
            t_ps = psum(ph, "t_ps")
            o_ps = psum(ph, "o_ps")
            m_ps = psum(ph, "m_ps")
            y_ps = psum(ph, "y_ps")

            s_bo = sem("x_bo_loaded")
            s_zero = sem("x_qbd_zeroed")
            s_raw = [sem(f"x_ctx_loaded{i}") for i in range(2)]
            s_ctx, s_rem = sem("x_ctx_split"), sem("x_ctx_rem_split")
            k_mm, k_hi_done, k_lo_done = sem("x_k_mm"), sem("x_k_hi"), sem("x_k_lo")
            v_mm, v_done = sem("x_v_mm"), sem("x_v_copied")
            q_mm, q_hi_done, q_done = sem("x_q_mm"), sem("x_q_hi"), sem("x_q_split")
            xt_mm, xt_hi_done, xt_done = sem("x_xt_mm"), sem("x_xt_hi"), sem("x_xt_split")
            s_mm, max_done, exp_done = sem("x_s_mm"), sem("x_max"), sem("x_exp")
            rinv_done, norm_done = sem("x_rinv"), sem("x_norm")
            t_mm, t_done = sem("x_t_mm"), sem("x_t_copied")
            pv_mm, ot_hi_done, ot_done = sem("x_pv_mm"), sem("x_ot_hi"), sem("x_ot_split")
            y_mm, y_added, bo_added = sem("x_y_mm"), sem("x_y_added"), sem("x_bo_added")

            LAG_S, LAG_T, LAG_PV = 1, 3, 4

            def run_tiles(eng, tile):
                for u in range(2):
                    tile(u, u, first=(u == 0), last=False, look=True)
                with eng.Fori(1, GROUPS - 1) as g:
                    for u in range(2):
                        tile(2 * g + u, u, first=False, last=False, look=True)
                for u in range(2):
                    tile(TILES - 2 + u, u, first=False, last=(u == 1), look=False)
                tile(TILES, 0, first=False, last=False, look=False, drain=True)

            block = ph.enter_context(nc.Block())

            @block.sync
            def _(sp):
                sp.dma_start(bo_b[:], bo.partition_broadcast(P)).then_inc(s_bo, DMA)

                def load(t, u):
                    wait(sp, s_ctx, 3 * (t - 1))
                    wait(sp, s_rem, t - 1)
                    sp.dma_start(ctx_raw[:, u, 0, :], ctx_t[t, 0:P, :]).then_inc(s_raw[u], DMA)
                    sp.dma_start(ctx_raw[0:REM, u, 1, :], ctx_t[t, P:C, :]).then_inc(s_raw[u], DMA)
                    sp.dma_start(ctx_raw[REM:P, u, 1, :], ctx_t[t, P:C, :]).then_inc(s_raw[u], DMA)

                for t in range(2):
                    load(t, t)
                with sp.Fori(1, GROUPS) as g:
                    for u in range(2):
                        load(2 * g + u, u)

            @block.gpsimd
            def _(pool):
                nc.gpsimd.memset(f32(qbd_hi[:]), 0.0).then_inc(s_zero, 1)
                nc.gpsimd.memset(f32(qbd_lo[:]), 0.0).then_inc(s_zero, 1)

                def split_part(t, u, part):
                    raw = ctx_raw[:, u]
                    if part == 0:
                        pool.wait_ge(s_raw[u], 3 * DMA * (t // 2 + 1))
                        wait(pool, v_mm, PAIRS * (t - 1))
                        round_pool(nc, cx_hi[:, u, :], raw[:, 0, :], zero).then_inc(s_ctx, 1)
                    if part == 1:
                        round_pool(nc, cx_rem[:, u, :], raw[:, 1, :], zero).then_inc(s_ctx, 1)
                    if part == 2:
                        pool.wait_ge(s_ctx, 3 * t + 1)
                        nc.gpsimd.tensor_tensor(cx_lo[:, u, :], raw[:, 0, :], f32(cx_hi[:, u, :]),
                                                ALU.subtract).then_inc(s_ctx, 1)

                def tile(t, u, first, last, look, drain=False):
                    for p in range(PAIRS):
                        n = PAIRS * t + p
                        if u == 0 and p == 1 and look:
                            ln_rstd(pool, ln, t // 2 + 1)
                        if (not first if p < LAG_S else not drain):
                            pool.wait_ge(rinv_done, n)
                            prob = p_sb[:, (p - 1) % 4, :].rearrange("p (b j) -> p b j", b=2)
                            inv = rinv[:, (p - 1) % 4, :].unsqueeze(2).to_broadcast([P, 2, J])
                            nc.gpsimd.tensor_tensor(prob, prob, inv, ALU.mult).then_inc(norm_done, 1)
                        if 1 <= p <= 3 and not last and not drain:
                            split_part(t + 1, 1 - u, p - 1)
                        if p == 6 and not first:
                            pool.wait_ge(y_added, t)
                            if isinstance(t, int) and t == 1:
                                pool.wait_ge(s_bo, DMA)
                            nc.gpsimd.tensor_tensor(x_sb[:, t - 1, :], x_sb[:, t - 1, :], bo_b[:],
                                                    ALU.add).then_inc(bo_added, 1)

                ln_rstd(pool, ln, 0)
                for part in range(3):
                    split_part(0, 0, part)
                run_tiles(pool, tile)

            @block.tensor
            def _(pe):
                def project_q(m, pair):
                    wait(pe, q_done, m)
                    c = slice(pair * P, (pair + 1) * P)
                    three_pass(pe, m_ps[:, 0:2 * P], [
                        x for d in range(DC) for x in hi_lo(wq_hi[:, d * E:][:, c], wq_lo[:, d * E:][:, c],
                                                            xt_hi[:, d, :], xt_lo[:, d, :])]).then_inc(q_mm, 1)

                def turn_x(g):
                    pe.wait_ge(ln["s_xn"], 2 * g + 2)
                    wait(pe, q_done, PAIRS * g)
                    for d in range(DC):
                        for u in range(2):
                            mm = pe.transpose(m_ps[:, (2 * d + u) * P:(2 * d + u + 1) * P],
                                              ln["xn"][:, u, d * P:(d + 1) * P], ident[:])
                    mm.then_inc(xt_mm, 1)

                def tile(t, u, first, last, look, drain=False):
                    for p in range(PAIRS):
                        n = PAIRS * t + p
                        cur, w = not drain, p % 2
                        if cur:
                            if p == 0:
                                pe.wait_ge(s_ctx, 3 * t + 3)
                                pe.wait_ge(s_rem, t + 1)
                            wait(pe, k_lo_done, n)
                            c0, c1 = slice(p * P, (p + 1) * P), slice(E + p * P, E + (p + 1) * P)
                            three_pass(pe, k_ps[:], hi_lo(wk_hi[:, c0], wk_lo[:, c0], cx_hi[:, u, :], cx_lo[:, u, :]) + [
                                (wk_hi[:, c1], cx_rem[:, u, :]), (wk_lo[:, c1], cx_rem[:, u, :])]).then_inc(k_mm, 1)
                        if (not first if p < LAG_S else cur):
                            q, uq = (p - 1) % PAIRS, (u if p else 1 - u)
                            wait(pe, k_lo_done, n)
                            if not drain:
                                wait(pe, q_done, PAIRS * (t // 2) + p if p else 0)
                            wait(pe, exp_done, n - 2)
                            for b in range(2):
                                keys = slice(b * J, (b + 1) * J)
                                mm = three_pass(pe, s_ps[1 - w][:, keys], hi_lo(
                                    qbd_hi[:, q, 2 * uq + b, :], qbd_lo[:, q, 2 * uq + b, :],
                                    kt_hi[:, 1 - w, keys], kt_lo[:, 1 - w, keys]))
                            mm.then_inc(s_mm, 1)
                        if u == 1 and p and look:
                            if p == 1:
                                pe.wait_ge(xt_done, t // 2 + 2)
                            project_q(PAIRS * (t // 2 + 1) + p - 1, p - 1)
                        if u == 0 and p == 0 and not first and cur:
                            project_q(PAIRS * (t // 2) + PAIRS - 1, PAIRS - 1)
                        if cur:
                            jt, half = p % 4, p // 4
                            wait(pe, v_done, n)
                            rows = slice(jt * P, (jt + 1) * P)
                            c0 = slice(half * HALF, (half + 1) * HALF)
                            c1 = slice(E + half * HALF, E + (half + 1) * HALF)
                            three_pass(pe, v_ps[:], hi_lo(cx_hi[:, u, rows], cx_lo[:, u, rows], wv_hi[:, c0], wv_lo[:, c0]) + [
                                (cx_rem[:, u, rows], wv_hi[:, c1]), (cx_rem[:, u, rows], wv_lo[:, c1])]).then_inc(v_mm, 1)
                        if (not first if p < LAG_T else cur):
                            pe.wait_ge(norm_done, n - 2)
                            wait(pe, t_done, n - 3)
                            for k in range(4):
                                mm = pe.transpose(t_ps[:, k * P:(k + 1) * P],
                                                  p_sb[:, (p - 3) % 4, k * P:(k + 1) * P], ident[:])
                            mm.then_inc(t_mm, 1)
                        if (not first if p < LAG_PV else cur):
                            q = (p - 4) % PAIRS
                            pe.wait_ge(t_done, n - 3)
                            pe.wait_ge(v_done, PAIRS * t + (4 if p >= LAG_PV else 0))
                            if w == 0:
                                wait(pe, ot_done, PAIRS // 2 * t + (p - 4) // 2)
                            for b in range(2):
                                for j in range(2):
                                    k = 2 * b + j
                                    mm = pe.matmul(o_ps[:, (2 * w + b) * P:(2 * w + b + 1) * P],
                                                   v_sb[:, k, q * P:(q + 1) * P], pt_sb[:, w, k * P:(k + 1) * P],
                                                   start=(j == 0), stop=(j == 1))
                            mm.then_inc(pv_mm, 1)
                        if p == 4 and not first:
                            pe.wait_ge(ot_done, PAIRS // 2 * t)
                            wait(pe, y_added, t - 1)
                            three_pass(pe, y_ps[:, 0:D], [
                                x for q in range(PAIRS) for x in hi_lo(
                                    ot_hi[:, q, :], ot_lo[:, q, :], wo_hi[:, q * D:(q + 1) * D],
                                    wo_lo[:, q * D:(q + 1) * D])]).then_inc(y_mm, 1)
                        if p == 4 and u == 0 and look:
                            turn_x(t // 2 + 1)

                turn_x(0)
                pe.wait_ge(xt_done, 1)
                for pair in range(PAIRS):
                    project_q(pair, pair)
                run_tiles(pe, tile)

            def heads(ps, qbd, pair, h):
                r = slice(h * HEAD, (h + 1) * HEAD)
                return (ps[r, 0:2 * P].rearrange("p (b q) -> p b q", b=4), qbd[r, pair, :, h * HEAD:(h + 1) * HEAD])

            def diag(h, w):
                r = slice(h * HEAD, (h + 1) * HEAD)
                return o_ps[r, :].rearrange("p (k q) -> p k q", k=4)[:, :, h * HEAD:(h + 1) * HEAD]

            def ot_part(ot, h, q):
                r = slice(h * HEAD, (h + 1) * HEAD)
                return ot[r, q - 1:q + 1, :].rearrange("p a (b q) -> p (a b) q", b=2)

            @block.scalar
            def _(act):
                def q_hi(m, pair, used):
                    act.wait_ge(q_mm, m + 1)
                    wait(act, s_mm, used)
                    for h in range(2):
                        src, dst = heads(m_ps, qbd_hi, pair, h)
                        split_hi_act(nc, dst, src, SCALE).then_inc(q_hi_done, 1)

                def xt_hi_copy(g):
                    act.wait_ge(xt_mm, g + 1)
                    wait(act, q_mm, PAIRS * g)
                    split_hi_act(nc, xt_hi[:].rearrange("p d t -> p (d t)"), m_ps[:]).then_inc(xt_hi_done, 1)

                def tile(t, u, first, last, look, drain=False):
                    for p in range(PAIRS):
                        n = PAIRS * t + p
                        cur, w = not drain, p % 2
                        if cur:
                            act.wait_ge(k_mm, n + 1)
                            wait(act, s_mm, n - 1)
                            split_hi_act(nc, kt_hi[:, w, :], k_ps[:]).then_inc(k_hi_done, 1)
                        if (not first if p < LAG_S else cur):
                            act.wait_ge(max_done, n)
                            wait(act, t_mm, n - 4)
                            k = (p - 1) % 4
                            for b in range(2):
                                ex = nc.scalar.activation(p_sb[:, k, b * J:(b + 1) * J], s_ps[1 - w][:, b * J:(b + 1) * J],
                                                          ACT.Exp, bias=nmax[:, k, b:b + 1], scale=1.0,
                                                          accum_out=rsum[:, k, b:b + 1])
                            ex.then_inc(exp_done, 1)
                        if u == 1 and p and look:
                            q_hi(PAIRS * (t // 2 + 1) + p - 1, p - 1, n)
                        if u == 0 and p == 0 and not first and cur:
                            q_hi(PAIRS * (t // 2) + PAIRS - 1, PAIRS - 1, n)
                        if cur:
                            act.wait_ge(v_mm, n + 1)
                            wait(act, pv_mm, PAIRS * t - (4 if p < 4 else 0))
                            nc.scalar.copy(v_sb[:, p % 4, p // 4 * HALF:(p // 4 + 1) * HALF], v_ps[:]).then_inc(v_done, 1)
                        if w == 1 and (not first if p < LAG_PV else cur):
                            act.wait_ge(pv_mm, n - 3)
                            if p >= LAG_PV:
                                wait(act, y_mm, t)
                            for h in range(2):
                                split_hi_act(nc, ot_part(ot_hi, h, (p - 4) % PAIRS), diag(h, w)).then_inc(ot_hi_done, 1)
                        if p == 4 and u == 0 and look:
                            xt_hi_copy(t // 2 + 1)

                xt_hi_copy(0)
                act.wait_ge(s_zero, 2)
                for pair in range(PAIRS):
                    q_hi(pair, pair, 0)
                run_tiles(act, tile)

            @block.vector
            def _(dve):
                def q_lo(m, pair):
                    dve.wait_ge(q_hi_done, 2 * m + 2)
                    for h in range(2):
                        src, dst = heads(m_ps, qbd_lo, pair, h)
                        _, hi = heads(m_ps, qbd_hi, pair, h)
                        lo = split_lo_dve(nc, dst, src, hi, SCALE)
                    lo.then_inc(q_done, 1)

                def xt_lo_copy(g):
                    dve.wait_ge(xt_hi_done, g + 1)
                    split_lo_dve(nc, xt_lo[:].rearrange("p d t -> p (d t)"), m_ps[:],
                                 xt_hi[:].rearrange("p d t -> p (d t)")).then_inc(xt_done, 1)

                def tile(t, u, first, last, look, drain=False):
                    for p in range(PAIRS):
                        n = PAIRS * t + p
                        cur, w = not drain, p % 2
                        if cur:
                            dve.wait_ge(k_hi_done, n + 1)
                            split_lo_dve(nc, kt_lo[:, w, :], k_ps[:], kt_hi[:, w, :]).then_inc(k_lo_done, 1)
                        if (not first if p < LAG_S else cur):
                            dve.wait_ge(s_mm, n)
                            nc.vector.tensor_reduce(nmax[:, (p - 1) % 4, :], s_ps[1 - w][:].rearrange("p (b j) -> p b j", b=2),
                                                    AX_X, ALU.max, negate=True).then_inc(max_done, 1)
                        if u == 1 and p and look:
                            q_lo(PAIRS * (t // 2 + 1) + p - 1, p - 1)
                        if u == 0 and p == 0 and not first and cur:
                            q_lo(PAIRS * (t // 2) + PAIRS - 1, PAIRS - 1)
                        if (not first if p < LAG_T else cur):
                            dve.wait_ge(t_mm, n - 2)
                            wait(dve, pv_mm, n - 4)
                            nc.vector.tensor_copy(pt_sb[:, 1 - w, :], t_ps[:]).then_inc(t_done, 1)
                        if (not first if p < LAG_S else cur):
                            dve.wait_ge(exp_done, n)
                            nc.vector.reciprocal(rinv[:, (p - 1) % 4, :], rsum[:, (p - 1) % 4, :]).then_inc(rinv_done, 1)
                        if w == 1 and (not first if p < LAG_PV else cur):
                            dve.wait_ge(ot_hi_done, PAIRS * t + p - 3)
                            q = (p - 4) % PAIRS
                            for h in range(2):
                                lo = split_lo_dve(nc, ot_part(ot_lo, h, q), diag(h, w), ot_part(ot_hi, h, q))
                            lo.then_inc(ot_done, 1)
                        if p == 5 and not first:
                            dve.wait_ge(y_mm, t)
                            nc.vector.tensor_tensor(x_sb[:, t - 1, :], y_ps[:, 0:D], x_sb[:, t - 1, :],
                                                    ALU.add).then_inc(y_added, 1)
                        if p == 6 and not last and not drain:
                            rem_lo(t + 1, 1 - u)
                        if p == 4 and u == 0 and look:
                            xt_lo_copy(t // 2 + 1)
                        if p == 0 and u == 0 and look:
                            ln_stats(dve, ln, t // 2 + 1)
                        if p == 2 and u == 0 and look:
                            wait(dve, xt_mm, t // 2 + 1)
                            ln_apply(dve, ln, t // 2 + 1)

                def rem_lo(t, u):
                    dve.wait_ge(s_ctx, 3 * t + 2)
                    split_lo_dve(nc, cx_rem[REM:P, u, :], ctx_raw[REM:P, u, 1, :], cx_rem[REM:P, u, :]).then_inc(s_rem, 1)

                ln_stats(dve, ln, 0)
                ln_apply(dve, ln, 0)
                rem_lo(0, 0)
                xt_lo_copy(0)
                dve.wait_ge(s_zero, 2)
                for pair in range(PAIRS):
                    q_lo(pair, pair)
                run_tiles(dve, tile)

        with ExitStack() as ph:
            wq_hi, wq_lo = pair_of(ph, "sq", DC * E)
            wk_hi, wk_lo = pair_of(ph, "sk", DC * E)
            wv_hi, wv_lo = pair_of(ph, "sv", DC * E)
            wo_hi, wo_lo = pair_of(ph, "so", PAIRS * D)
            load_weights("s", [([(0, P, 0, 2048, w.rearrange("(c p) n -> p c n", p=P))], 2048, hi[:], lo[:])
                               for w, hi, lo in ((sq, wq_hi, wq_lo), (sk, wk_hi, wk_lo),
                                                 (sv, wv_hi, wv_lo), (so, wo_hi, wo_lo))])

            xt_hi = sbuf(ph, "sxt_hi", [P, DC, 2 * P], F32R)
            xt_lo = sbuf(ph, "sxt_lo", [P, DC, 2 * P], F32R)
            qt_hi = sbuf(ph, "sqt_hi", [P, 2, 2 * P], F32R)
            qt_lo = sbuf(ph, "sqt_lo", [P, 2, 2 * P], F32R)
            kbd_hi = sbuf(ph, "skbd_hi", [P, 2, 2, 2, P], F32R)
            kbd_lo = sbuf(ph, "skbd_lo", [P, 2, 2, 2, P], F32R)
            v_sb = sbuf(ph, "sv_sb", [P, 2, E])
            sm_sb = sbuf(ph, "sm_sb", [P, 2, HALF])
            p_sb = sbuf(ph, "sp_sb", [P, 4, HALF])
            pt_sb = sbuf(ph, "spt_sb", [P, 2, HALF])
            ot_hi = sbuf(ph, "sot_hi", [P, PAIRS, 2 * P], F32R)
            ot_lo = sbuf(ph, "sot_lo", [P, PAIRS, 2 * P], F32R)
            nmax = sbuf(ph, "snmax", [P, 4, 4])
            rsum = sbuf(ph, "srsum", [P, 4, 4])
            rinv = sbuf(ph, "srinv", [P, 4, 4])
            ln = ln_buffers(ph, "s")

            qk_ps = psum(ph, "sqk_ps")
            v_ps = psum(ph, "sv_ps")
            s_ps = [psum(ph, f"ss_ps{i}") for i in range(2)]
            t_ps = psum(ph, "st_ps")
            o_ps = psum(ph, "so_ps")
            m_ps = psum(ph, "sm_ps")
            y_ps = psum(ph, "sy_ps")

            s_zero = sem("s_kbd_zeroed")
            qk_mm, qk_hi_done, qk_done = sem("s_qk_mm"), sem("s_qk_hi"), sem("s_qk_split")
            v_mm, v_done = sem("s_v_mm"), sem("s_v_copied")
            xt_mm, xt_hi_done, xt_done = sem("s_xt_mm"), sem("s_xt_hi"), sem("s_xt_split")
            s_mm, sm_done, max_done, exp_done = sem("s_s_mm"), sem("s_masked"), sem("s_max"), sem("s_exp")
            rinv_done, norm_done = sem("s_rinv"), sem("s_norm")
            t_mm, t_done = sem("s_t_mm"), sem("s_t_copied")
            pv_mm, ot_hi_done, ot_done = sem("s_pv_mm"), sem("s_ot_hi"), sem("s_ot_split")
            y_mm, y_added = sem("s_y_mm"), sem("s_y_added")

            LAG_S, LAG_T, LAG_PV = 1, 3, 4

            def run_groups(eng, group):
                group(0, first=True, look=True)
                with eng.Fori(1, GROUPS - 1) as g:
                    group(g, first=False, look=True)
                group(GROUPS - 1, first=False, look=False)
                group(GROUPS, first=False, look=False, drain=True)

            block = ph.enter_context(nc.Block())

            @block.gpsimd
            def _(pool):
                nc.gpsimd.memset(f32(kbd_hi[:]), 0.0).then_inc(s_zero, 1)
                nc.gpsimd.memset(f32(kbd_lo[:]), 0.0).then_inc(s_zero, 1)

                def group(g, first, look, drain=False):
                    for p in range(PAIRS):
                        n = PAIRS * g + p
                        if p == 1 and look:
                            ln_rstd(pool, ln, g + 1)
                        if (not first if p < LAG_S else not drain):
                            pool.wait_ge(rinv_done, n)
                            prob = p_sb[:, (p - 1) % 4, :].rearrange("p (k j) -> p k j", k=4)
                            inv = rinv[:, (p - 1) % 4, :].unsqueeze(2).to_broadcast([P, 4, P])
                            nc.gpsimd.tensor_tensor(prob, prob, inv, ALU.mult).then_inc(norm_done, 1)

                ln_rstd(pool, ln, 0)
                run_groups(pool, group)

            @block.tensor
            def _(pe):
                def turn_x(g):
                    pe.wait_ge(ln["s_xn"], 2 * g + 2)
                    wait(pe, xt_done, g)
                    for d in range(DC):
                        for u in range(2):
                            mm = pe.transpose(m_ps[:, (2 * d + u) * P:(2 * d + u + 1) * P],
                                              ln["xn"][:, u, d * P:(d + 1) * P], ident[:])
                    mm.then_inc(xt_mm, 1)

                def group(g, first, look, drain=False):
                    for p in range(PAIRS):
                        n = PAIRS * g + p
                        cur, w = not drain, p % 2
                        if cur:
                            if p == 0:
                                pe.wait_ge(xt_done, g + 1)
                            wait(pe, qk_done, n)
                            for i, (hi, lo) in enumerate(((wq_hi, wq_lo), (wk_hi, wk_lo))):
                                mm = three_pass(pe, qk_ps[:, i * 2 * P:(i + 1) * 2 * P], [
                                    x for d in range(DC) for x in hi_lo(
                                        hi[:, d * E + p * P:d * E + (p + 1) * P], lo[:, d * E + p * P:d * E + (p + 1) * P],
                                        xt_hi[:, d, :], xt_lo[:, d, :])])
                            mm.then_inc(qk_mm, 1)
                        if p == PAIRS - 1 and look:
                            turn_x(g + 1)
                        if (not first if p < LAG_S else cur):
                            wait(pe, qk_done, n)
                            wait(pe, sm_done, n - 2)
                            for u in range(2):
                                keys = lambda kbd: kbd[:, 1 - w, u, :, :].rearrange("p h j -> p (h j)")
                                rows = slice(u * P, (u + 1) * P)
                                mm = three_pass(pe, s_ps[1 - w][:, u * 2 * P:(u + 1) * 2 * P], hi_lo(
                                    qt_hi[:, 1 - w, rows], qt_lo[:, 1 - w, rows], keys(kbd_hi), keys(kbd_lo)))
                            mm.then_inc(s_mm, 1)
                        if cur and p % 4 < 2:
                            i = 4 * g + p // 4 * 2 + p % 4
                            wait(pe, v_done, i)
                            half, rows = p // 4, slice(p % 4 * P, (p % 4 + 1) * P)
                            three_pass(pe, v_ps[:], [
                                x for d in range(DC) for x in hi_lo(
                                    xt_hi[:, d, rows], xt_lo[:, d, rows],
                                    wv_hi[:, d * E + half * HALF:d * E + (half + 1) * HALF],
                                    wv_lo[:, d * E + half * HALF:d * E + (half + 1) * HALF])]).then_inc(v_mm, 1)
                        if (not first if p < LAG_T else cur):
                            pe.wait_ge(norm_done, n - 2)
                            wait(pe, t_done, n - 3)
                            for k in range(4):
                                mm = pe.transpose(t_ps[:, k * P:(k + 1) * P],
                                                  p_sb[:, (p - 3) % 4, k * P:(k + 1) * P], ident[:])
                            mm.then_inc(t_mm, 1)
                        if (not first if p < LAG_PV else cur):
                            q = (p - 4) % PAIRS
                            pe.wait_ge(t_done, n - 3)
                            pe.wait_ge(v_done, 4 * g + (2 if p >= LAG_PV else 0))
                            if w == 0:
                                wait(pe, ot_done, PAIRS // 2 * g + (p - 4) // 2)
                            for u in range(2):
                                for h in range(2):
                                    k = 2 * u + h
                                    mm = pe.matmul(o_ps[h * HEAD:(h + 1) * HEAD, (2 * w + u) * P:(2 * w + u + 1) * P],
                                                   v_sb[:, u, q * P + h * HEAD:q * P + (h + 1) * HEAD],
                                                   pt_sb[:, w, k * P:(k + 1) * P], start=True, stop=True)
                            mm.then_inc(pv_mm, 1)
                        if p == 4 and not first:
                            pe.wait_ge(ot_done, PAIRS // 2 * g)
                            wait(pe, y_added, g - 1)
                            for u in range(2):
                                mm = three_pass(pe, y_ps[:, u * D:(u + 1) * D], [
                                    x for q in range(PAIRS) for x in hi_lo(
                                        ot_hi[:, q, u * P:(u + 1) * P], ot_lo[:, q, u * P:(u + 1) * P],
                                        wo_hi[:, q * D:(q + 1) * D], wo_lo[:, q * D:(q + 1) * D])])
                            mm.then_inc(y_mm, 1)

                turn_x(0)
                run_groups(pe, group)

            def k_part(kbd, w, h):
                r = slice(h * HEAD, (h + 1) * HEAD)
                return (qk_ps[r, 2 * P:4 * P].rearrange("p (u j) -> p u j", u=2), kbd[r, w, :, h, :])

            @block.scalar
            def _(act):
                def xt_hi_copy(g):
                    act.wait_ge(xt_mm, g + 1)
                    wait(act, qk_mm, PAIRS * g)
                    wait(act, v_mm, 4 * g)
                    split_hi_act(nc, xt_hi[:].rearrange("p d t -> p (d t)"), m_ps[:]).then_inc(xt_hi_done, 1)

                def group(g, first, look, drain=False):
                    for p in range(PAIRS):
                        n = PAIRS * g + p
                        cur, w = not drain, p % 2
                        if cur:
                            act.wait_ge(qk_mm, n + 1)
                            wait(act, s_mm, n - 1)
                            split_hi_act(nc, qt_hi[:, w, :], qk_ps[:, 0:2 * P], SCALE).then_inc(qk_hi_done, 1)
                            for h in range(2):
                                src, dst = k_part(kbd_hi, w, h)
                                split_hi_act(nc, dst, src).then_inc(qk_hi_done, 1)
                        if p == PAIRS - 1 and look:
                            xt_hi_copy(g + 1)
                        if (not first if p < LAG_S else cur):
                            act.wait_ge(max_done, n)
                            wait(act, t_mm, n - 4)
                            s = (p - 1) % 4
                            for k in range(4):
                                ex = nc.scalar.activation(p_sb[:, s, k * P:(k + 1) * P], sm_sb[:, 1 - w, k * P:(k + 1) * P],
                                                          ACT.Exp, bias=nmax[:, s, k:k + 1], scale=1.0,
                                                          accum_out=rsum[:, s, k:k + 1])
                            ex.then_inc(exp_done, 1)
                        if cur and p % 4 < 2:
                            i = 4 * g + p // 4 * 2 + p % 4
                            act.wait_ge(v_mm, i + 1)
                            wait(act, pv_mm, PAIRS * g - (4 if p < 4 else 0))
                            nc.scalar.copy(v_sb[:, p % 4, p // 4 * HALF:(p // 4 + 1) * HALF], v_ps[:]).then_inc(v_done, 1)
                        if w == 1 and (not first if p < LAG_PV else cur):
                            q = (p - 4) % PAIRS
                            act.wait_ge(pv_mm, n - 3)
                            if p >= LAG_PV:
                                wait(act, y_mm, g)
                            split_hi_act(nc, ot_hi[:, q - 1:q + 1, :].rearrange("p a t -> p (a t)"),
                                         o_ps[:]).then_inc(ot_hi_done, 1)

                xt_hi_copy(0)
                act.wait_ge(s_zero, 2)
                run_groups(act, group)

            @block.vector
            def _(dve):
                def xt_lo_copy(g):
                    dve.wait_ge(xt_hi_done, g + 1)
                    split_lo_dve(nc, xt_lo[:].rearrange("p d t -> p (d t)"), m_ps[:],
                                 xt_hi[:].rearrange("p d t -> p (d t)")).then_inc(xt_done, 1)

                def group(g, first, look, drain=False):
                    for p in range(PAIRS):
                        n = PAIRS * g + p
                        cur, w = not drain, p % 2
                        if cur:
                            dve.wait_ge(qk_hi_done, 3 * n + 3)
                            split_lo_dve(nc, qt_lo[:, w, :], qk_ps[:, 0:2 * P], qt_hi[:, w, :], SCALE)
                            for h in range(2):
                                src, dst = k_part(kbd_lo, w, h)
                                lo = split_lo_dve(nc, dst, src, k_part(kbd_hi, w, h)[1])
                            lo.then_inc(qk_done, 1)
                        if p == PAIRS - 1 and look:
                            xt_lo_copy(g + 1)
                        if (not first if p < LAG_S else cur):
                            dve.wait_ge(s_mm, n)
                            wait(dve, exp_done, n - 2)
                            nc.vector.tensor_tensor(sm_sb[:, 1 - w, :], s_ps[1 - w][:],
                                                    mask[:].rearrange("p k j -> p (k j)"), ALU.add).then_inc(sm_done, 1)
                            dve.wait_ge(sm_done, n)
                            nc.vector.tensor_reduce(nmax[:, (p - 1) % 4, :], sm_sb[:, 1 - w, :].rearrange("p (k j) -> p k j", k=4),
                                                    AX_X, ALU.max, negate=True).then_inc(max_done, 1)
                        if (not first if p < LAG_T else cur):
                            dve.wait_ge(t_mm, n - 2)
                            wait(dve, pv_mm, n - 4)
                            nc.vector.tensor_copy(pt_sb[:, 1 - w, :], t_ps[:]).then_inc(t_done, 1)
                        if (not first if p < LAG_S else cur):
                            dve.wait_ge(exp_done, n)
                            nc.vector.reciprocal(rinv[:, (p - 1) % 4, :], rsum[:, (p - 1) % 4, :]).then_inc(rinv_done, 1)
                        if w == 1 and (not first if p < LAG_PV else cur):
                            q = (p - 4) % PAIRS
                            dve.wait_ge(ot_hi_done, PAIRS // 2 * g + (p - 3) // 2)
                            split_lo_dve(nc, ot_lo[:, q - 1:q + 1, :].rearrange("p a t -> p (a t)"), o_ps[:],
                                         ot_hi[:, q - 1:q + 1, :].rearrange("p a t -> p (a t)")).then_inc(ot_done, 1)
                        if p == 5 and not first:
                            dve.wait_ge(y_mm, g)
                            tiles = x_sb[:, bass.ds(2 * g - 2, 2), :].rearrange("p u d -> p (u d)")
                            nc.vector.tensor_tensor(tiles, y_ps[:], tiles, ALU.add).then_inc(y_added, 1)
                        if p == 0 and look:
                            ln_stats(dve, ln, g + 1)
                        if p == 2 and look:
                            wait(dve, xt_mm, g + 1)
                            ln_apply(dve, ln, g + 1)

                ln_stats(dve, ln, 0)
                ln_apply(dve, ln, 0)
                xt_lo_copy(0)
                run_groups(dve, group)

        moe(nc, root, sem, sbuf, psum, load_weights, ln_buffers, ln_stats, ln_rstd, ln_apply,
            x_sb, ident, zero, router, w_gate, w_up, w_down, out)


def moe(nc, root, sem, sbuf, psum, load_weights, ln_buffers, ln_stats, ln_rstd, ln_apply,
        x_sb, ident, zero, router, w_gate, w_up, w_down, out):
    _, TILES, D = x_sb.shape
    DC = D // P
    GROUPS = TILES // 2
    EXPERTS, _, F = w_gate.shape
    FC = F // P
    BLOCKS = TILES // 4
    TB = 4 * P
    GU = DC * F

    with ExitStack() as ph:
        xt_hi = sbuf(ph, "fxt_hi", [P, DC, TILES * P], F32R)
        xt_lo = sbuf(ph, "fxt_lo", [P, DC, TILES * P], F32R)
        weight = sbuf(ph, "f_weight", [P, TILES, EXPERTS])

        with ExitStack() as rt:
            r_raw = sbuf(rt, "r_raw", [P, DC, EXPERTS])
            r_hi = sbuf(rt, "r_hi", [P, DC, P], F32R)
            r_lo = sbuf(rt, "r_lo", [P, DC, P], F32R)
            lt_sb = sbuf(rt, "lt_sb", [P, 2, 2 * P])
            logit = sbuf(rt, "logit", [P, TILES, EXPERTS])
            prob = sbuf(rt, "prob", [P, TILES, EXPERTS])
            tmp = sbuf(rt, "r_tmp", [P, TILES, EXPERTS])
            hot = [sbuf(rt, f"hot{i}", [P, TILES, EXPERTS]) for i in range(2)]
            rank = sbuf(rt, "rank", [P, TILES, EXPERTS])
            col = [sbuf(rt, f"r_col{i}", [P, TILES]) for i in range(6)]
            ln = ln_buffers(rt, "f")
            xt_ps = [psum(rt, f"fxt_ps{i}") for i in range(2)]
            lt_ps = psum(rt, "flt_ps")
            lg_ps = psum(rt, "flg_ps")
            s_router, s_rz, s_rh, s_rl = sem("f_router"), sem("f_rz"), sem("f_rh"), sem("f_rl")
            s_rank = sem("f_rank")
            xt_mm, xt_h, xt_l = sem("f_xt_mm"), sem("f_xt_hi"), sem("f_xt_split")
            lt_mm, lt_done, lg_mm, lg_done = sem("f_lt_mm"), sem("f_lt_copied"), sem("f_lg_mm"), sem("f_lg_copied")
            chain, s_exp = sem("f_chain"), sem("f_exp")
            LOGIT_MINUS_MAX, SECOND_MINUS_FIRST = 2, 16

            block = rt.enter_context(nc.Block())

            @block.sync
            def _(sp):
                sp.dma_start(r_raw[:], router.rearrange("(c p) e -> p c e", p=P)).then_inc(s_router, DMA)

            @block.gpsimd
            def _(pool):
                nc.gpsimd.memset(f32(r_hi[:]), 0.0).then_inc(s_rz, 1)
                nc.gpsimd.memset(f32(r_lo[:]), 0.0).then_inc(s_rz, 1)
                for e in range(EXPERTS):
                    nc.gpsimd.memset(rank[:, :, e:e + 1], float(EXPERTS - e)).then_inc(s_rank, 1)
                ln_rstd(pool, ln, 0)
                with pool.Fori(1, GROUPS) as g:
                    ln_rstd(pool, ln, g)

            @block.tensor
            def _(pe):
                def group(g, w):
                    pe.wait_ge(ln["s_xn"], 2 * g + 2)
                    wait(pe, xt_l, g - 1)
                    for d in range(DC):
                        for u in range(2):
                            mm = pe.transpose(xt_ps[w][:, (2 * d + u) * P:(2 * d + u + 1) * P],
                                              ln["xn"][:, u, d * P:(d + 1) * P], ident[:])
                    mm.then_inc(xt_mm, 1)

                def logits(g, w):
                    pe.wait_ge(xt_l, g + 1)
                    wait(pe, lt_done, g)
                    rows = bass.ds(g * 2 * P, 2 * P)
                    three_pass(pe, lt_ps[:, 0:2 * P], [
                        x for d in range(DC) for x in hi_lo(r_hi[:, d, :], r_lo[:, d, :],
                                                            xt_hi[:, d, rows], xt_lo[:, d, rows])]).then_inc(lt_mm, 1)
                    pe.wait_ge(lt_done, g + 1)
                    wait(pe, lg_done, g)
                    for u in range(2):
                        mm = pe.transpose(lg_ps[:, u * P:(u + 1) * P], lt_sb[:, w, u * P:(u + 1) * P], ident[:])
                    mm.then_inc(lg_mm, 1)

                pe.wait_ge(s_rl, 1)
                for g in range(2):
                    group(g, g)
                    logits(g, g)
                with pe.Fori(1, GROUPS // 2) as i:
                    for u in range(2):
                        group(2 * i + u, u)
                        logits(2 * i + u, u)

            def rows(g):
                return bass.ds(g * 2 * P, 2 * P)

            @block.scalar
            def _(act):
                act.wait_ge(s_router, DMA)
                act.wait_ge(s_rz, 2)
                nc.scalar.copy(r_hi[:, :, 0:EXPERTS], r_raw[:]).then_inc(s_rh, 1)

                def group(g, w):
                    act.wait_ge(xt_mm, g + 1)
                    split_hi_act(nc, xt_hi[:, :, rows(g)], xt_ps[w][:].rearrange("p (d t) -> p d t", d=DC)).then_inc(xt_h, 1)
                    act.wait_ge(lt_mm, g + 1)
                    wait(act, lg_mm, g - 1)
                    nc.scalar.copy(lt_sb[:, w, :], lt_ps[:, 0:2 * P]).then_inc(lt_done, 1)

                for g in range(2):
                    group(g, g)
                with act.Fori(1, GROUPS // 2) as i:
                    for u in range(2):
                        group(2 * i + u, u)
                act.wait_ge(chain, LOGIT_MINUS_MAX)
                nc.scalar.activation(prob[:], tmp[:], ACT.Exp).then_inc(s_exp, 1)
                act.wait_ge(chain, SECOND_MINUS_FIRST)
                nc.scalar.activation(col[4][:], col[3][:], ACT.Exp).then_inc(s_exp, 1)

            @block.vector
            def _(dve):
                dve.wait_ge(s_rh, 1)
                nc.vector.tensor_tensor(r_lo[:, :, 0:EXPERTS], r_raw[:], f32(r_hi[:, :, 0:EXPERTS]),
                                        ALU.subtract).then_inc(s_rl, 1)

                def group(g, w):
                    ln_stats(dve, ln, g)
                    wait(dve, xt_mm, g)
                    ln_apply(dve, ln, g)
                    dve.wait_ge(xt_h, g + 1)
                    split_lo_dve(nc, xt_lo[:, :, rows(g)], xt_ps[w][:].rearrange("p (d t) -> p d t", d=DC),
                                 xt_hi[:, :, rows(g)]).then_inc(xt_l, 1)
                    dve.wait_ge(lg_mm, g + 1)
                    nc.vector.tensor_copy(logit[:, bass.ds(2 * g, 2), :],
                                          lg_ps[:, 0:2 * P].rearrange("p (u e) -> p u e", u=2)[:, :, 0:EXPERTS]).then_inc(lg_done, 1)

                for g in range(2):
                    group(g, g)
                with dve.Fori(1, GROUPS // 2) as i:
                    for u in range(2):
                        group(2 * i + u, u)

                count = [0]

                def link(ins):
                    count[0] += 1
                    ins.then_inc(chain, 1)
                    dve.wait_ge(chain, count[0])

                def wide(c):
                    return c[:].unsqueeze(2).to_broadcast([P, TILES, EXPERTS])

                dve.wait_ge(lg_done, GROUPS)
                dve.wait_ge(s_rank, EXPERTS)
                V = nc.vector
                link(V.tensor_reduce(col[0][:], logit[:], AX_X, ALU.max))
                link(V.tensor_tensor(tmp[:], logit[:], wide(col[0]), ALU.subtract))
                dve.wait_ge(s_exp, 1)
                link(V.tensor_reduce(col[0][:], prob[:], AX_X, ALU.add))
                link(V.reciprocal(col[1][:], col[0][:]))
                link(V.tensor_tensor(prob[:], prob[:], wide(col[1]), ALU.mult))
                for k in range(2):
                    link(V.tensor_reduce(col[1 + k][:], prob[:], AX_X, ALU.max))
                    link(V.tensor_tensor(tmp[:], prob[:], wide(col[1 + k]), ALU.is_equal))
                    link(V.tensor_tensor(tmp[:], tmp[:], rank[:], ALU.mult))
                    link(V.tensor_reduce(col[0][:], tmp[:], AX_X, ALU.max))
                    if k == 0:
                        link(V.tensor_tensor(hot[k][:], tmp[:], wide(col[0]), ALU.is_equal))
                        link(V.scalar_tensor_tensor(out=prob[:].rearrange("p t e -> p (t e)"),
                                                    in0=hot[k][:].rearrange("p t e -> p (t e)"), scalar=-2.0,
                                                    in1=prob[:].rearrange("p t e -> p (t e)"), op0=ALU.mult, op1=ALU.add))
                link(V.tensor_tensor(col[3][:], col[2][:], col[1][:], ALU.subtract))
                assert count[0] == SECOND_MINUS_FIRST
                link(V.tensor_tensor(hot[1][:], tmp[:], wide(col[0]), ALU.is_equal))
                dve.wait_ge(s_exp, 2)
                link(V.tensor_scalar(col[5][:], col[4][:], 1.0, None, ALU.add))
                link(V.reciprocal(col[0][:], col[5][:]))
                link(V.tensor_tensor(col[1][:], col[4][:], col[0][:], ALU.mult))
                link(V.tensor_tensor(hot[0][:], hot[0][:], wide(col[0]), ALU.mult))
                link(V.tensor_tensor(hot[1][:], hot[1][:], wide(col[1]), ALU.mult))
                link(V.tensor_tensor(weight[:], hot[0][:], hot[1][:], ALU.add))

        raw = sbuf(ph, "e_raw", [P, 2 * GU + FC * D])
        w_hi = sbuf(ph, "e_hi", [P, 2, 2 * GU + FC * D], F32R)
        w_lo = sbuf(ph, "e_lo", [P, 2, 2 * GU + FC * D], F32R)
        act_sb = sbuf(ph, "e_act", [P, 2, TB])
        h_sb = sbuf(ph, "e_h", [P, 2, TB])
        h_hi = sbuf(ph, "e_h_hi", [P, FC, TB], F32R)
        h_lo = sbuf(ph, "e_h_lo", [P, FC, TB], F32R)
        g_ps = [psum(ph, f"g_ps{i}") for i in range(2)]
        u_ps = [psum(ph, f"u_ps{i}") for i in range(2)]
        y_ps = [psum(ph, f"e_y_ps{i}") for i in range(4)]
        s_raw, s_whi, s_wlo = sem("e_raw_loaded"), sem("e_w_hi"), sem("e_w_split")
        gu_mm, silu_done, prod_done, hhi_done, h_done = (sem("e_gu_mm"), sem("e_silu"), sem("e_prod"),
                                                         sem("e_h_hi_done"), sem("e_h_split"))
        y_mm, y_added, s_out = sem("e_y_mm"), sem("e_y_added"), sem("out_stored")

        block = ph.enter_context(nc.Block())

        @block.sync
        def _(sp):
            def load(e):
                wait(sp, s_wlo, e)
                sp.dma_start(raw[:, 0:GU].rearrange("p (c f) -> p c f", c=DC),
                             w_gate[e].rearrange("(c p) f -> p c f", p=P)).then_inc(s_raw, DMA)
                sp.dma_start(raw[:, GU:2 * GU].rearrange("p (c f) -> p c f", c=DC),
                             w_up[e].rearrange("(c p) f -> p c f", p=P)).then_inc(s_raw, DMA)
                sp.dma_start(raw[:, 2 * GU:].rearrange("p (c d) -> p c d", c=FC),
                             w_down[e].rearrange("(c p) d -> p c d", p=P)).then_inc(s_raw, DMA)

            for e in range(EXPERTS):
                load(e)
            sp.wait_ge(y_added, EXPERTS * BLOCKS * 4)
            sp.dma_start(out.rearrange("(t p) d -> p t d", p=P), x_sb[:]).then_inc(s_out, DMA)
            sp.wait_ge(s_out, DMA)

        @block.gpsimd
        def _(pool):
            for e in range(EXPERTS):
                pool.wait_ge(s_raw, 3 * DMA * (e + 1))
                wait(pool, y_mm, 4 * BLOCKS * (e - 1))
                round_pool(nc, w_hi[:, e % 2, :], raw[:], zero).then_inc(s_whi, 1)
                pool.wait_ge(s_whi, e + 1)
                nc.gpsimd.tensor_tensor(w_lo[:, e % 2, :], raw[:], f32(w_hi[:, e % 2, :]), ALU.subtract).then_inc(s_wlo, 1)

        def run_blocks(eng, body):
            def expert(e, w):
                with eng.Fori(0, BLOCKS) as b:
                    body(e, w, b, e * BLOCKS + b)

            for e in range(EXPERTS):
                if e == 0:
                    body(0, 0, 0, 0)
                    with eng.Fori(1, BLOCKS) as b:
                        body(0, 0, b, b)
                else:
                    expert(e, e % 2)

        @block.tensor
        def _(pe):
            def body(e, w, b, i):
                tok = bass.ds(b * TB, TB)

                def gate_up(f):
                    for s, ps in ((0, g_ps[f % 2]), (1, u_ps[f % 2])):
                        cols = [slice(s * GU + d * F + f * P, s * GU + d * F + (f + 1) * P) for d in range(DC)]
                        mm = three_pass(pe, ps[:], [x for d in range(DC) for x in hi_lo(
                            w_hi[:, w, cols[d]], w_lo[:, w, cols[d]], xt_hi[:, d, tok], xt_lo[:, d, tok])])
                    mm.then_inc(gu_mm, 1)

                def down(f):
                    pe.wait_ge(h_done, FC * i + f + 1)
                    c = slice(2 * GU + f * D, 2 * GU + (f + 1) * D)
                    for j in range(4):
                        if f == 0:
                            wait(pe, y_added, 4 * i - 3 + j)
                        for k, (a, m) in enumerate(hi_lo(h_hi[:, f, j * P:(j + 1) * P], h_lo[:, f, j * P:(j + 1) * P],
                                                         w_hi[:, w, c], w_lo[:, w, c])):
                            mm = pe.matmul(y_ps[j][:, 0:D], a, m, start=(f == 0 and k == 0), stop=(f == FC - 1 and k == 2))
                        if f == FC - 1:
                            mm.then_inc(y_mm, 1)

                pe.wait_ge(s_wlo, e + 1)
                for f in range(FC):
                    wait(pe, prod_done, FC * i + f - 1)
                    gate_up(f)
                    if f:
                        down(f - 1)
                down(FC - 1)

            run_blocks(pe, body)

        @block.scalar
        def _(act):
            def body(e, w, b, i):
                for f in range(FC):
                    act.wait_ge(gu_mm, FC * i + f + 1)
                    wait(act, prod_done, FC * i + f - 1)
                    nc.scalar.activation(act_sb[:, f % 2, :], g_ps[f % 2][:], ACT.Silu).then_inc(silu_done, 1)
                    act.wait_ge(prod_done, FC * i + f + 1)
                    wait(act, y_mm, 4 * i)
                    split_hi_act(nc, h_hi[:, f, :], h_sb[:, f % 2, :]).then_inc(hhi_done, 1)

            run_blocks(act, body)

        @block.vector
        def _(dve):
            def body(e, w, b, i):
                for f in range(FC):
                    dve.wait_ge(silu_done, FC * i + f + 1)
                    wait(dve, h_done, FC * i + f - 1)
                    nc.vector.tensor_tensor(h_sb[:, f % 2, :], u_ps[f % 2][:], act_sb[:, f % 2, :],
                                            ALU.mult).then_inc(prod_done, 1)
                    dve.wait_ge(hhi_done, FC * i + f + 1)
                    split_lo_dve(nc, h_lo[:, f, :], h_sb[:, f % 2, :], h_hi[:, f, :]).then_inc(h_done, 1)
                for j in range(4):
                    dve.wait_ge(y_mm, 4 * i + j + 1)
                    t = 4 * b + j
                    nc.vector.scalar_tensor_tensor(
                        out=x_sb[:, bass.ds(t, 1), :].rearrange("p a d -> p (a d)"), in0=y_ps[j][:, 0:D],
                        scalar=weight[:, bass.ds(t, 1), e:e + 1].rearrange("p a b -> p (a b)"),
                        in1=x_sb[:, bass.ds(t, 1), :].rearrange("p a d -> p (a d)"),
                        op0=ALU.mult, op1=ALU.add).then_inc(y_added, 1)

            run_blocks(dve, body)


def kernel(**inputs):
    import numpy as np
    import concourse.bacc as bacc
    from concourse.bass_utils import run_bass_kernel_spmd

    a = {k: np.asarray(v) for k, v in inputs.items()}
    x = a["x"]
    B, S, D = x.shape
    _, J, C = a["ctx_768"].shape
    tiles = B * S // P
    arrays = {
        "x": x.reshape(B * S, D),
        "ctx_t": a["ctx_768"].reshape(tiles, 2 * J, C).transpose(0, 2, 1),
        "xattn_wq": a["L0_xattn_Wq"], "xattn_wk": a["L0_xattn_Wk"], "xattn_wv": a["L0_xattn_Wv"],
        "xattn_wo": a["L0_xattn_Wo"], "xattn_bo": a["L0_xattn_bo"],
        "attn_wq": a["L0_attn_wq"].T, "attn_wk": a["L0_attn_wk"].T, "attn_wv": a["L0_attn_wv"].T,
        "attn_wo": a["L0_attn_wo"].T,
        "router": a["L0_ffn_router_kernel_DE"], "gate": a["L0_ffn_kernel_gating_EDF"],
        "up": a["L0_ffn_kernel_up_EDF"], "down": a["L0_ffn_kernel_down_EFD"],
    }
    nc = bacc.Bacc("TRN2", target_bir_lowering=False, num_devices=1)
    feed, args = {}, []
    for name, arr in arrays.items():
        arr = np.ascontiguousarray(arr)
        feed["in_" + name] = arr
        args.append(nc.dram_tensor("in_" + name, arr.shape, mybir.dt.from_np(arr.dtype), kind="ExternalInput").ap())
    args.append(nc.dram_tensor("out_x", (B * S, D), F32, kind="ExternalOutput").ap())
    layer_kernel(nc, *args)
    r = run_bass_kernel_spmd(nc, [feed], core_ids=[0])
    return r.results[0]["out_x"].reshape(B, S, D)
```

```python
from contextlib import ExitStack

import concourse.bass as bass
from concourse import mybir

ALU = mybir.AluOpType
ACT = mybir.ActivationFunctionType
AX_X = mybir.AxisListType.X
F32 = mybir.dt.float32
F32R = mybir.dt.float32r

P = 128
HEAD = 64
MIN_TILES = 5
EPS = 1e-5
MASKED = -1e30
DMA = 16


def wait(eng, sem, value):
    if isinstance(value, int) and value <= 0:
        return
    eng.wait_ge(sem, value)


def f32(ap):
    return ap.bitcast(F32)


def split_hi_act(nc, hi, src, scale=None):
    if scale is None:
        return nc.scalar.copy(hi, src)
    return nc.scalar.mul(hi, src, scale)


def round_pool(nc, hi, src, zero):
    return nc.gpsimd.tensor_tensor(hi, src, zero[:].to_broadcast(list(src.shape)), ALU.add)


def split_lo_dve(nc, lo, src, hi, scale=None):
    if scale is None:
        return nc.vector.tensor_tensor(lo, src, f32(hi), ALU.subtract)
    return nc.vector.scalar_tensor_tensor(out=lo, in0=src, scalar=scale, in1=f32(hi),
                                          op0=ALU.mult, op1=ALU.subtract)


def three_pass(pe, out, pairs):
    for i, (lhs, rhs) in enumerate(pairs):
        mm = pe.matmul(out, lhs, rhs, start=(i == 0), stop=(i == len(pairs) - 1))
    return mm


def hi_lo(a_hi, a_lo, b_hi, b_lo):
    return [(a_hi, b_hi), (a_lo, b_hi), (a_hi, b_lo)]


def layer_kernel(nc, x, ctx_t, wq, wk, wv, wo, bo, sq, sk, sv, so, router, w_gate, w_up, w_down, out):
    NTOK, D = x.shape
    TILES = NTOK // P
    DC = D // P
    _, C, TJ = ctx_t.shape
    J = TJ // 2
    REM = C - P
    E = wq.shape[1]
    PAIRS = E // P
    GROUPS = TILES // 2
    STEPS = TILES * PAIRS
    EXPERTS, _, F = w_gate.shape
    FC = F // P
    HALF = 512
    SCALE = HEAD ** -0.5
    assert REM == HEAD and DC == 2 and PAIRS == 8 and HALF == 2 * J and E == 2 * HALF

    with ExitStack() as root:
        def sem(name):
            return root.enter_context(nc.semaphore(name))

        def sbuf(stack, name, shape, dt=F32):
            return stack.enter_context(nc.sbuf_tensor(name, shape, dt))

        def psum(stack, name, shape=(P, HALF)):
            return stack.enter_context(nc.psum_tensor(name, list(shape), F32))

        x_sb = sbuf(root, "x_sb", [P, TILES, D])
        ident = sbuf(root, "ident", [P, P])
        mask = sbuf(root, "mask", [P, 4, P])
        neg_half = sbuf(root, "neg_half", [P, 2])
        zero = sbuf(root, "zero", [P, 1])

        class Weights:

            def __init__(self, phase, jobs):
                self.jobs = jobs
                self.loaded = [sem(f"w_loaded_{phase}_{i}") for i in range(len(jobs))]
                self.his, self.los = sem(f"w_hi_{phase}"), sem(f"w_lo_{phase}")

            def load(self, sp, n):
                for dst, src in self.jobs[n][0]:
                    sp.dma_start(dst, src).then_inc(self.loaded[n], DMA)

            def split_hi(self, act, n):
                dmas, stage, hi, lo = self.jobs[n]
                act.wait_ge(self.loaded[n], DMA * len(dmas))
                split_hi_act(nc, hi, stage).then_inc(self.his, 1)

            def split_lo(self, dve, n):
                dmas, stage, hi, lo = self.jobs[n]
                dve.wait_ge(self.his, n + 1)
                split_lo_dve(nc, lo, stage, hi).then_inc(self.los, 1)

            def wait_split(self, eng, jobs):
                eng.wait_ge(self.los, jobs)

        def plain_jobs(w, hi, lo, stages):
            w = w.rearrange("(c p) n -> p c n", p=P)
            half = w.shape[1] // 2
            return [([(st.rearrange("p (c n) -> p c n", c=half), w[:, i * half:(i + 1) * half, :])], st,
                     hi[:, i * E:(i + 1) * E], lo[:, i * E:(i + 1) * E]) for i, st in enumerate(stages)]

        def pair_of(stack, name, cols):
            return (sbuf(stack, name + "_hi", [P, cols], F32R), sbuf(stack, name + "_lo", [P, cols], F32R))

        def ln_buffers(stack, phase):
            return dict(
                stats=sbuf(stack, f"ln_stats_{phase}", [P, 2, 6]),
                mv=sbuf(stack, f"ln_mv_{phase}", [P, 2, 2]),
                veps=sbuf(stack, f"ln_veps_{phase}", [P, 2]),
                rstd=sbuf(stack, f"ln_rstd_{phase}", [P, 2]),
                xn=sbuf(stack, f"ln_xn_{phase}", [P, 2, D]),
                gate=sbuf(stack, f"ln_gate_{phase}", [P, 1]), s_gate=sem(f"ln_gate_done_{phase}"),
                s_stats=sem(f"ln_stats_done_{phase}"), s_mv=sem(f"ln_mv_done_{phase}"),
                s_veps=sem(f"ln_veps_done_{phase}"), s_rstd=sem(f"ln_rstd_done_{phase}"),
                s_xn=sem(f"ln_xn_done_{phase}"))

        def ln_stats(dve, ln, g):
            wait(dve, ln["s_xn"], 2 * g)
            for u in range(2):
                nc.vector.bn_stats(ln["stats"][:, u, :], x_sb[:, 2 * g + u, :]).then_inc(ln["s_stats"], 1)
            wait(dve, ln["s_gate"], g)
            dve.wait_ge(ln["s_stats"], 2 * g + 2)
            nc.vector.memset(ln["gate"][:], 0.0).then_inc(ln["s_gate"], 1)
            for u in range(2):
                nc.vector.bn_aggr(ln["mv"][:, u, :], ln["stats"][:, u, :]).then_inc(ln["s_mv"], 1)
            dve.wait_ge(ln["s_mv"], 2 * g + 2)
            nc.vector.tensor_scalar(ln["veps"][:], ln["mv"][:, :, 1], EPS, None, ALU.add).then_inc(ln["s_veps"], 1)

        def ln_rstd(pool, ln, g):
            pool.wait_ge(ln["s_veps"], g + 1)
            nc.gpsimd.tensor_tensor(ln["rstd"][:], ln["veps"][:], neg_half[:], ALU.pow).then_inc(ln["s_rstd"], 1)

        def ln_apply(dve, ln, g, into=None):
            dve.wait_ge(ln["s_rstd"], g + 1)
            for u in range(2):
                dst = ln["xn"][:, u, :] if into is None else into[:, 2 * g + u, :]
                nc.vector.tensor_scalar(dst, x_sb[:, 2 * g + u, :], ln["mv"][:, u, 0:1],
                                        ln["rstd"][:, u:u + 1], ALU.subtract, ALU.mult).then_inc(ln["s_xn"], 1)

        MAX_TILES = 2 * TILES + 1 + (EXPERTS - 2) * MIN_TILES
        SLOT_TILES = MAX_TILES + 1
        FILLS = 8
        assert SLOT_TILES % FILLS == 0
        slots = nc.dram_tensor("slots", (SLOT_TILES * P, D), F32, kind="Internal").ap()
        xn_dram = nc.dram_tensor("xn", (NTOK, D), F32, kind="Internal").ap()
        blank = sbuf(root, "blank", [P, D])
        s_fill = sem("slots_filled")
        s_x = [sem("x_first_loaded"), sem("x_rest_loaded")]
        X_FIRST = 4
        x_dram = x.rearrange("(t p) d -> p t d", p=P)
        s_const = sem("const_ready")
        with nc.Block() as block:
            @block.gpsimd
            def _(pool):
                nc.gpsimd.memset(blank[:], 0.0).then_inc(s_const, 1)
                nc.gpsimd.memset(ident[:], 0.0).then_inc(s_const, 1)
                nc.gpsimd.memset(mask[:], 0.0).then_inc(s_const, 1)
                nc.gpsimd.memset(neg_half[:], -0.5).then_inc(s_const, 1)
                nc.gpsimd.memset(zero[:], 0.0).then_inc(s_const, 1)
                pool.wait_ge(s_const, 5)
                nc.gpsimd.affine_select(out=ident[:], in_=ident[:], compare_op=ALU.not_equal, fill=1.0, base=0,
                                        pattern=[[-1, P]], channel_multiplier=1).then_inc(s_const, 1)
                nc.gpsimd.affine_select(out=mask[:], in_=mask[:], compare_op=ALU.is_ge, fill=MASKED, base=0,
                                        pattern=[[0, 4], [-1, P]], channel_multiplier=1).then_inc(s_const, 1)
                pool.wait_ge(s_const, 7)
                nc.gpsimd.memset(mask[HEAD:P, :, 0:HEAD], MASKED).then_inc(s_const, 1)
                pool.wait_ge(s_const, 8)

        with ExitStack() as ph:
            bo_b = sbuf(ph, "bo_b", [P, D])
            wq_hi, wq_lo = pair_of(ph, "wq", DC * E)
            wk_hi, wk_lo = pair_of(ph, "wk", 2 * E)
            wv_hi, wv_lo = pair_of(ph, "wv", 2 * E)
            wo_hi, wo_lo = pair_of(ph, "wo", PAIRS * D)

            ctx_raw = sbuf(ph, "ctx_raw", [P, 2, 2, HALF])
            cx_hi = sbuf(ph, "cx_hi", [P, 2, HALF], F32R)
            cx_lo = sbuf(ph, "cx_lo", [P, 2, HALF], F32R)
            cx_rem = sbuf(ph, "cx_rem", [P, 2, HALF], F32R)
            qbd_hi = sbuf(ph, "qbd_hi", [P, PAIRS, 4, P], F32R)
            qbd_lo = sbuf(ph, "qbd_lo", [P, PAIRS, 4, P], F32R)
            kt_hi = sbuf(ph, "kt_hi", [P, 2, HALF], F32R)
            kt_lo = sbuf(ph, "kt_lo", [P, 2, HALF], F32R)
            v_sb = sbuf(ph, "v_sb", [P, 4, E])
            p_sb = sbuf(ph, "p_sb", [P, 4, HALF])
            pt_sb = sbuf(ph, "pt_sb", [P, 2, HALF])
            ot_hi = sbuf(ph, "ot_hi", [P, PAIRS, P], F32R)
            ot_lo = sbuf(ph, "ot_lo", [P, PAIRS, P], F32R)
            xt_hi = sbuf(ph, "xt_hi", [P, DC, 2 * P], F32R)
            xt_lo = sbuf(ph, "xt_lo", [P, DC, 2 * P], F32R)
            nmax = sbuf(ph, "nmax", [P, 4, 2])
            rsum = sbuf(ph, "rsum", [P, 4, 2])
            rinv = sbuf(ph, "rinv", [P, 4, 2])
            ln = ln_buffers(ph, "x")

            def jobs_192(w, hi, lo, stages):
                return [([(stages[0], w[0:P, :])], stages[0], hi[:, 0:E], lo[:, 0:E]),
                        ([(stages[1][0:REM], w[P:C, :]), (stages[1][REM:P], w[P:C, :])], stages[1],
                         hi[:, E:2 * E], lo[:, E:2 * E])]

            p_flat = p_sb[:].rearrange("p k j -> p (k j)")
            weights = Weights("x", plain_jobs(wq, wq_hi, wq_lo, [v_sb[:, i, :] for i in range(2)])
                              + jobs_192(wk, wk_hi, wk_lo, [v_sb[:, i, :] for i in range(2, 4)])
                              + jobs_192(wv, wv_hi, wv_lo, [p_flat[:, i * E:(i + 1) * E] for i in range(2)])
                              + plain_jobs(wo, wo_hi, wo_lo, [b.rearrange("p k j -> p (k j)") for b in (pt_sb[:], ctx_raw[:, 1])]))
            Q_SPLIT, K_SPLIT, V_SPLIT, O_SPLIT = 2, 4, 6, 8

            k_ps = psum(ph, "k_ps")
            v_ps = psum(ph, "v_ps")
            s_ps = [psum(ph, f"s_ps{i}") for i in range(2)]
            t_ps = psum(ph, "t_ps")
            o_ps = psum(ph, "o_ps")
            m_ps = psum(ph, "m_ps")
            y_ps = psum(ph, "y_ps")

            s_bo = sem("x_bo_loaded")
            s_zero = sem("x_qbd_zeroed")
            s_raw = [sem(f"x_ctx_loaded{i}") for i in range(2)]
            s_ctx, s_rem = sem("x_ctx_split"), sem("x_ctx_rem_split")
            k_mm, k_hi_done, k_lo_done = sem("x_k_mm"), sem("x_k_hi"), sem("x_k_lo")
            v_mm, v_done = sem("x_v_mm"), sem("x_v_copied")
            q_mm, q_hi_done, q_done = sem("x_q_mm"), sem("x_q_hi"), sem("x_q_split")
            xt_mm, xt_hi_done, xt_done = sem("x_xt_mm"), sem("x_xt_hi"), sem("x_xt_split")
            s_mm, max_done, exp_done = sem("x_s_mm"), sem("x_max"), sem("x_exp")
            rinv_done, norm_done = sem("x_rinv"), sem("x_norm")
            t_mm, t_done = sem("x_t_mm"), sem("x_t_copied")
            pv_mm, ot_hi_done, ot_done = sem("x_pv_mm"), sem("x_ot_hi"), sem("x_ot_split")
            y_mm, y_added, bo_added = sem("x_y_mm"), sem("x_y_added"), sem("x_bo_added")

            LAG_S, LAG_T, LAG_PV = 1, 3, 4

            def run_tiles(eng, tile):
                for u in range(2):
                    tile(u, u, first=(u == 0), last=False, look=True)
                with eng.Fori(1, GROUPS - 1) as g:
                    for u in range(2):
                        tile(2 * g + u, u, first=False, last=False, look=True)
                for u in range(2):
                    tile(TILES - 2 + u, u, first=False, last=(u == 1), look=False)
                tile(TILES, 0, first=False, last=False, look=False, drain=True)

            block = ph.enter_context(nc.Block())

            @block.sync
            def _(sp):
                def load(t, u):
                    wait(sp, s_ctx, 3 * (t - 1))
                    wait(sp, s_rem, t - 1)
                    sp.dma_start(ctx_raw[:, u, 0, :], ctx_t[t, 0:P, :]).then_inc(s_raw[u], DMA)
                    sp.dma_start(ctx_raw[0:REM, u, 1, :], ctx_t[t, P:C, :]).then_inc(s_raw[u], DMA)
                    sp.dma_start(ctx_raw[REM:P, u, 1, :], ctx_t[t, P:C, :]).then_inc(s_raw[u], DMA)

                sp.dma_start(x_sb[:, 0:X_FIRST, :], x_dram[:, 0:X_FIRST, :]).then_inc(s_x[0], DMA)
                for n in range(Q_SPLIT):
                    weights.load(sp, n)
                load(0, 0)
                for n in range(Q_SPLIT, O_SPLIT):
                    weights.load(sp, n)
                weights.wait_split(sp, O_SPLIT)
                load(1, 1)
                sp.dma_start(x_sb[:, X_FIRST:, :], x_dram[:, X_FIRST:, :]).then_inc(s_x[1], DMA)
                sp.dma_start(bo_b[:], bo.partition_broadcast(P)).then_inc(s_bo, DMA)
                fill = SLOT_TILES // FILLS
                with sp.Fori(1, FILLS + 1) as g:
                    for u in range(2):
                        load(2 * g + u, u)
                    sp.dma_start(slots.rearrange("(t p) d -> p t d", p=P)[:, bass.ds(fill * g - fill, fill), :],
                                 blank[:].unsqueeze(1).to_broadcast([P, fill, D])).then_inc(s_fill, DMA)
                with sp.Fori(FILLS + 1, GROUPS) as g:
                    for u in range(2):
                        load(2 * g + u, u)

            @block.gpsimd
            def _(pool):
                nc.gpsimd.memset(f32(qbd_hi[:]), 0.0).then_inc(s_zero, 1)
                nc.gpsimd.memset(f32(qbd_lo[:]), 0.0).then_inc(s_zero, 1)

                def split_part(t, u, part):
                    raw = ctx_raw[:, u]
                    if part == 0:
                        pool.wait_ge(s_raw[u], 3 * DMA * (t // 2 + 1))
                        wait(pool, v_mm, PAIRS * (t - 1))
                        round_pool(nc, cx_hi[:, u, :], raw[:, 0, :], zero).then_inc(s_ctx, 1)
                    if part == 1:
                        round_pool(nc, cx_rem[:, u, :], raw[:, 1, :], zero).then_inc(s_ctx, 1)
                    if part == 2:
                        pool.wait_ge(s_ctx, 3 * t + 1)
                        nc.gpsimd.tensor_tensor(cx_lo[:, u, :], raw[:, 0, :], f32(cx_hi[:, u, :]),
                                                ALU.subtract).then_inc(s_ctx, 1)

                def tile(t, u, first, last, look, drain=False):
                    for p in range(PAIRS):
                        n = PAIRS * t + p
                        if u == 0 and p == 1 and look:
                            ln_rstd(pool, ln, t // 2 + 1)
                        if (not first if p < LAG_S else not drain):
                            pool.wait_ge(rinv_done, n)
                            prob = p_sb[:, (p - 1) % 4, :].rearrange("p (b j) -> p b j", b=2)
                            inv = rinv[:, (p - 1) % 4, :].unsqueeze(2).to_broadcast([P, 2, J])
                            nc.gpsimd.tensor_tensor(prob, prob, inv, ALU.mult).then_inc(norm_done, 1)
                        if 1 <= p <= 3 and not last and not drain:
                            split_part(t + 1, 1 - u, p - 1)
                        if p == 6 and not first:
                            pool.wait_ge(y_added, t)
                            if isinstance(t, int) and t == 1:
                                pool.wait_ge(s_bo, DMA)
                            nc.gpsimd.tensor_tensor(x_sb[:, t - 1, :], x_sb[:, t - 1, :], bo_b[:],
                                                    ALU.add).then_inc(bo_added, 1)

                ln_rstd(pool, ln, 0)
                for part in range(3):
                    split_part(0, 0, part)
                run_tiles(pool, tile)

            @block.tensor
            def _(pe):
                def project_q(m, pair):
                    wait(pe, q_done, m)
                    c = slice(pair * P, (pair + 1) * P)
                    three_pass(pe, m_ps[:, 0:2 * P], [
                        x for d in range(DC) for x in hi_lo(wq_hi[:, d * E:][:, c], wq_lo[:, d * E:][:, c],
                                                            xt_hi[:, d, :], xt_lo[:, d, :])]).then_inc(q_mm, 1)

                def turn_x(g):
                    pe.wait_ge(ln["s_xn"], 2 * g + 2)
                    wait(pe, q_done, PAIRS * g)
                    for d in range(DC):
                        for u in range(2):
                            mm = pe.transpose(m_ps[:, (2 * d + u) * P:(2 * d + u + 1) * P],
                                              ln["xn"][:, u, d * P:(d + 1) * P], ident[:])
                    mm.then_inc(xt_mm, 1)

                def tile(t, u, first, last, look, drain=False):
                    for p in range(PAIRS):
                        n = PAIRS * t + p
                        cur, w = not drain, p % 2
                        if cur:
                            if p == 0 and first:
                                weights.wait_split(pe, K_SPLIT)
                            if p == 0:
                                pe.wait_ge(s_ctx, 3 * t + 3)
                                pe.wait_ge(s_rem, t + 1)
                            wait(pe, k_lo_done, n)
                            c0, c1 = slice(p * P, (p + 1) * P), slice(E + p * P, E + (p + 1) * P)
                            three_pass(pe, k_ps[:], hi_lo(wk_hi[:, c0], wk_lo[:, c0], cx_hi[:, u, :], cx_lo[:, u, :]) + [
                                (wk_hi[:, c1], cx_rem[:, u, :]), (wk_lo[:, c1], cx_rem[:, u, :])]).then_inc(k_mm, 1)
                        if (not first if p < LAG_S else cur):
                            q, uq = (p - 1) % PAIRS, (u if p else 1 - u)
                            wait(pe, k_lo_done, n)
                            if not drain:
                                wait(pe, q_done, PAIRS * (t // 2) + p if p else 0)
                                if p == 0 and u == 1 and isinstance(t, int) and look:
                                    pe.wait_ge(q_done, PAIRS)
                            wait(pe, exp_done, n - 2)
                            for b in range(2):
                                keys = slice(b * J, (b + 1) * J)
                                mm = three_pass(pe, s_ps[1 - w][:, keys], hi_lo(
                                    qbd_hi[:, q, 2 * uq + b, :], qbd_lo[:, q, 2 * uq + b, :],
                                    kt_hi[:, 1 - w, keys], kt_lo[:, 1 - w, keys]))
                            mm.then_inc(s_mm, 1)
                        if first:
                            project_q(p, p)
                            if p == 0:
                                weights.wait_split(pe, V_SPLIT)
                        if p == 0 and u == 1 and isinstance(t, int) and look:
                            turn_x(1)
                        if u == 1 and p and look:
                            if p == 1:
                                pe.wait_ge(xt_done, t // 2 + 2)
                            project_q(PAIRS * (t // 2 + 1) + p - 1, p - 1)
                        if u == 0 and p == 0 and not first and cur:
                            project_q(PAIRS * (t // 2) + PAIRS - 1, PAIRS - 1)
                        if cur:
                            jt, half = p % 4, p // 4
                            wait(pe, v_done, n)
                            rows = slice(jt * P, (jt + 1) * P)
                            c0 = slice(half * HALF, (half + 1) * HALF)
                            c1 = slice(E + half * HALF, E + (half + 1) * HALF)
                            three_pass(pe, v_ps[:], hi_lo(cx_hi[:, u, rows], cx_lo[:, u, rows], wv_hi[:, c0], wv_lo[:, c0]) + [
                                (cx_rem[:, u, rows], wv_hi[:, c1]), (cx_rem[:, u, rows], wv_lo[:, c1])]).then_inc(v_mm, 1)
                        if (not first if p < LAG_T else cur):
                            pe.wait_ge(norm_done, n - 2)
                            wait(pe, t_done, n - 3)
                            for k in range(4):
                                mm = pe.transpose(t_ps[:, k * P:(k + 1) * P],
                                                  p_sb[:, (p - 3) % 4, k * P:(k + 1) * P], ident[:])
                            mm.then_inc(t_mm, 1)
                        if (not first if p < LAG_PV else cur):
                            q = (p - 4) % PAIRS
                            pe.wait_ge(t_done, n - 3)
                            pe.wait_ge(v_done, PAIRS * t + (4 if p >= LAG_PV else 0))
                            if w == 0:
                                wait(pe, ot_done, PAIRS // 2 * t + (p - 4) // 2)
                            for b in range(2):
                                for j in range(2):
                                    k = 2 * b + j
                                    mm = pe.matmul(o_ps[:, (2 * w + b) * P:(2 * w + b + 1) * P],
                                                   v_sb[:, k, q * P:(q + 1) * P], pt_sb[:, w, k * P:(k + 1) * P],
                                                   start=(j == 0), stop=(j == 1))
                            mm.then_inc(pv_mm, 1)
                        if p == 4 and not first:
                            if isinstance(t, int) and t == 1:
                                weights.wait_split(pe, O_SPLIT)
                            pe.wait_ge(ot_done, PAIRS // 2 * t)
                            wait(pe, y_added, t - 1)
                            three_pass(pe, y_ps[:, 0:D], [
                                x for q in range(PAIRS) for x in hi_lo(
                                    ot_hi[:, q, :], ot_lo[:, q, :], wo_hi[:, q * D:(q + 1) * D],
                                    wo_lo[:, q * D:(q + 1) * D])]).then_inc(y_mm, 1)
                        if p == 4 and u == 0 and look and not first:
                            turn_x(t // 2 + 1)

                turn_x(0)
                weights.wait_split(pe, Q_SPLIT)
                pe.wait_ge(xt_done, 1)
                run_tiles(pe, tile)

            def heads(ps, qbd, pair, h):
                r = slice(h * HEAD, (h + 1) * HEAD)
                return (ps[r, 0:2 * P].rearrange("p (b q) -> p b q", b=4), qbd[r, pair, :, h * HEAD:(h + 1) * HEAD])

            def diag(h, w):
                r = slice(h * HEAD, (h + 1) * HEAD)
                return o_ps[r, :].rearrange("p (k q) -> p k q", k=4)[:, :, h * HEAD:(h + 1) * HEAD]

            def ot_part(ot, h, q):
                r = slice(h * HEAD, (h + 1) * HEAD)
                return ot[r, q - 1:q + 1, :].rearrange("p a (b q) -> p (a b) q", b=2)

            @block.scalar
            def _(act):
                def q_hi(m, pair, used):
                    act.wait_ge(q_mm, m + 1)
                    wait(act, s_mm, used)
                    for h in range(2):
                        src, dst = heads(m_ps, qbd_hi, pair, h)
                        split_hi_act(nc, dst, src, SCALE).then_inc(q_hi_done, 1)

                def xt_hi_copy(g):
                    act.wait_ge(xt_mm, g + 1)
                    wait(act, q_mm, PAIRS * g)
                    split_hi_act(nc, xt_hi[:].rearrange("p d t -> p (d t)"), m_ps[:]).then_inc(xt_hi_done, 1)

                def tile(t, u, first, last, look, drain=False):
                    for p in range(PAIRS):
                        n = PAIRS * t + p
                        cur, w = not drain, p % 2
                        if cur:
                            act.wait_ge(k_mm, n + 1)
                            wait(act, s_mm, n - 1)
                            split_hi_act(nc, kt_hi[:, w, :], k_ps[:]).then_inc(k_hi_done, 1)
                        if (not first if p < LAG_S else cur):
                            act.wait_ge(max_done, n)
                            wait(act, t_mm, n - 4)
                            if first and p == 1:
                                weights.wait_split(act, V_SPLIT)
                            k = (p - 1) % 4
                            for b in range(2):
                                ex = nc.scalar.activation(p_sb[:, k, b * J:(b + 1) * J], s_ps[1 - w][:, b * J:(b + 1) * J],
                                                          ACT.Exp, bias=nmax[:, k, b:b + 1], scale=1.0,
                                                          accum_out=rsum[:, k, b:b + 1])
                            ex.then_inc(exp_done, 1)
                        if first:
                            q_hi(p, p, 0)
                            if p == 1:
                                weights.split_hi(act, V_SPLIT)
                                weights.split_hi(act, V_SPLIT + 1)
                        if p == 0 and u == 1 and isinstance(t, int) and look:
                            xt_hi_copy(1)
                        if u == 1 and p and look:
                            q_hi(PAIRS * (t // 2 + 1) + p - 1, p - 1, n)
                        if u == 0 and p == 0 and not first and cur:
                            q_hi(PAIRS * (t // 2) + PAIRS - 1, PAIRS - 1, n)
                        if cur:
                            act.wait_ge(v_mm, n + 1)
                            wait(act, pv_mm, PAIRS * t - (4 if p < 4 else 0))
                            if first and p == 0:
                                weights.wait_split(act, K_SPLIT)
                            nc.scalar.copy(v_sb[:, p % 4, p // 4 * HALF:(p // 4 + 1) * HALF], v_ps[:]).then_inc(v_done, 1)
                        if w == 1 and (not first if p < LAG_PV else cur):
                            act.wait_ge(pv_mm, n - 3)
                            if p >= LAG_PV:
                                wait(act, y_mm, t)
                            for h in range(2):
                                split_hi_act(nc, ot_part(ot_hi, h, (p - 4) % PAIRS), diag(h, w)).then_inc(ot_hi_done, 1)
                        if p == 4 and u == 0 and look and not first:
                            xt_hi_copy(t // 2 + 1)

                xt_hi_copy(0)
                for n in range(V_SPLIT):
                    weights.split_hi(act, n)
                act.wait_ge(s_zero, 2)
                run_tiles(act, tile)

            @block.vector
            def _(dve):
                def q_lo(m, pair):
                    dve.wait_ge(q_hi_done, 2 * m + 2)
                    for h in range(2):
                        src, dst = heads(m_ps, qbd_lo, pair, h)
                        _, hi = heads(m_ps, qbd_hi, pair, h)
                        lo = split_lo_dve(nc, dst, src, hi, SCALE)
                    lo.then_inc(q_done, 1)

                def xt_lo_copy(g):
                    dve.wait_ge(xt_hi_done, g + 1)
                    split_lo_dve(nc, xt_lo[:].rearrange("p d t -> p (d t)"), m_ps[:],
                                 xt_hi[:].rearrange("p d t -> p (d t)")).then_inc(xt_done, 1)

                def tile(t, u, first, last, look, drain=False):
                    for p in range(PAIRS):
                        n = PAIRS * t + p
                        cur, w = not drain, p % 2
                        if cur:
                            dve.wait_ge(k_hi_done, n + 1)
                            split_lo_dve(nc, kt_lo[:, w, :], k_ps[:], kt_hi[:, w, :]).then_inc(k_lo_done, 1)
                        if (not first if p < LAG_S else cur):
                            dve.wait_ge(s_mm, n)
                            nc.vector.tensor_reduce(nmax[:, (p - 1) % 4, :], s_ps[1 - w][:].rearrange("p (b j) -> p b j", b=2),
                                                    AX_X, ALU.max, negate=True).then_inc(max_done, 1)
                        if first:
                            q_lo(p, p)
                            if p == 1:
                                weights.split_lo(dve, V_SPLIT)
                                weights.split_lo(dve, V_SPLIT + 1)
                        if p == 0 and u == 1 and isinstance(t, int) and look:
                            xt_lo_copy(1)
                        if u == 1 and p and look:
                            q_lo(PAIRS * (t // 2 + 1) + p - 1, p - 1)
                        if u == 0 and p == 0 and not first and cur:
                            q_lo(PAIRS * (t // 2) + PAIRS - 1, PAIRS - 1)
                        if (not first if p < LAG_T else cur):
                            dve.wait_ge(t_mm, n - 2)
                            wait(dve, pv_mm, n - 4)
                            nc.vector.tensor_copy(pt_sb[:, 1 - w, :], t_ps[:]).then_inc(t_done, 1)
                        if (not first if p < LAG_S else cur):
                            dve.wait_ge(exp_done, n)
                            nc.vector.reciprocal(rinv[:, (p - 1) % 4, :], rsum[:, (p - 1) % 4, :]).then_inc(rinv_done, 1)
                        if w == 1 and (not first if p < LAG_PV else cur):
                            dve.wait_ge(ot_hi_done, PAIRS * t + p - 3)
                            q = (p - 4) % PAIRS
                            for h in range(2):
                                lo = split_lo_dve(nc, ot_part(ot_lo, h, q), diag(h, w), ot_part(ot_hi, h, q))
                            lo.then_inc(ot_done, 1)
                        if p == 5 and not first:
                            dve.wait_ge(y_mm, t)
                            nc.vector.tensor_tensor(x_sb[:, t - 1, :], y_ps[:, 0:D], x_sb[:, t - 1, :],
                                                    ALU.add).then_inc(y_added, 1)
                        if p == 6 and not last and not drain:
                            rem_lo(t + 1, 1 - u)
                        if p == 4 and u == 0 and look and not first:
                            xt_lo_copy(t // 2 + 1)
                        if p == 7 and u == 1 and isinstance(t, int) and look:
                            dve.wait_ge(s_x[1], DMA)
                        if p == 0 and u == 0 and look:
                            ln_stats(dve, ln, t // 2 + 1)
                        if p == 2 and u == 0 and look:
                            wait(dve, xt_mm, t // 2 + 1)
                            ln_apply(dve, ln, t // 2 + 1)

                def rem_lo(t, u):
                    dve.wait_ge(s_ctx, 3 * t + 2)
                    split_lo_dve(nc, cx_rem[REM:P, u, :], ctx_raw[REM:P, u, 1, :], cx_rem[REM:P, u, :]).then_inc(s_rem, 1)

                dve.wait_ge(s_x[0], DMA)
                ln_stats(dve, ln, 0)
                ln_apply(dve, ln, 0)
                xt_lo_copy(0)
                for n in range(Q_SPLIT):
                    weights.split_lo(dve, n)
                rem_lo(0, 0)
                for n in range(Q_SPLIT, V_SPLIT):
                    weights.split_lo(dve, n)
                dve.wait_ge(s_zero, 2)
                run_tiles(dve, tile)

        xn_sb = sbuf(root, "f_xn", [P, TILES, D])
        s_xn_stored = sem("f_xn_stored")
        r_raw = sbuf(root, "r_raw", [P, DC, EXPERTS])
        r_hi = sbuf(root, "r_hi", [P, DC, P], F32R)
        r_lo = sbuf(root, "r_lo", [P, DC, P], F32R)
        s_router, s_rz, s_rh, s_rl = sem("router_loaded"), sem("router_zeroed"), sem("router_hi"), sem("router_split")
        with ExitStack() as ph:
            wq_hi, wq_lo = pair_of(ph, "sq", DC * E)
            wk_hi, wk_lo = pair_of(ph, "sk", DC * E)
            wv_hi, wv_lo = pair_of(ph, "sv", DC * E)
            wo_hi, wo_lo = pair_of(ph, "so", PAIRS * D)
            xt_hi = sbuf(ph, "sxt_hi", [P, 2, DC, 2 * P], F32R)
            xt_lo = sbuf(ph, "sxt_lo", [P, 2, DC, 2 * P], F32R)
            qt_hi = sbuf(ph, "sqt_hi", [P, 2, 2 * P], F32R)
            qt_lo = sbuf(ph, "sqt_lo", [P, 2, 2 * P], F32R)
            kbd_hi = sbuf(ph, "skbd_hi", [P, 2, 2, 2, P], F32R)
            kbd_lo = sbuf(ph, "skbd_lo", [P, 2, 2, 2, P], F32R)
            v_sb = sbuf(ph, "sv_sb", [P, 2, E])
            sm_sb = sbuf(ph, "sm_sb", [P, 2, HALF])
            p_sb = sbuf(ph, "sp_sb", [P, 4, HALF])
            pt_sb = sbuf(ph, "spt_sb", [P, 2, HALF])
            ot_hi = sbuf(ph, "sot_hi", [P, PAIRS, 2 * P], F32R)
            ot_lo = sbuf(ph, "sot_lo", [P, PAIRS, 2 * P], F32R)
            nmax = sbuf(ph, "snmax", [P, 4, 4])
            rsum = sbuf(ph, "srsum", [P, 4, 4])
            rinv = sbuf(ph, "srinv", [P, 4, 4])
            ln = ln_buffers(ph, "s")
            ln_f = ln_buffers(ph, "f")

            stage = sbuf(ph, "s_stage", [P, 2 * E])
            p_flat = p_sb[:].rearrange("p k j -> p (k j)")
            flat_halves = lambda a: [a[:, i * E:(i + 1) * E] for i in range(2)]
            weights = Weights("s", plain_jobs(sq, wq_hi, wq_lo, flat_halves(p_flat))
                              + plain_jobs(sk, wk_hi, wk_lo, [b[:].rearrange("p k j -> p (k j)") for b in (sm_sb, pt_sb)])
                              + plain_jobs(sv, wv_hi, wv_lo, [v_sb[:, i, :] for i in range(2)])
                              + plain_jobs(so, wo_hi, wo_lo, flat_halves(stage[:])))
            Q_SPLIT, K_SPLIT, V_SPLIT, O_SPLIT = 2, 4, 6, 8

            qk_ps = [psum(ph, f"sqk_ps{i}") for i in range(2)]
            v_ps = psum(ph, "sv_ps")
            s_ps = [psum(ph, f"ss_ps{i}") for i in range(2)]
            t_ps = psum(ph, "st_ps")
            o_ps = psum(ph, "so_ps")
            y_ps = psum(ph, "sy_ps")

            s_zero = sem("s_kbd_zeroed")
            qk_mm, qk_hi_done, qk_done = sem("s_qk_mm"), sem("s_qk_hi"), sem("s_qk_split")
            v_mm, v_done = sem("s_v_mm"), sem("s_v_copied")
            xt_mm, xt_hi_done, xt_done = sem("s_xt_mm"), sem("s_xt_hi"), sem("s_xt_split")
            s_mm, sm_done, max_done, exp_done = sem("s_s_mm"), sem("s_masked"), sem("s_max"), sem("s_exp")
            rinv_done, norm_done = sem("s_rinv"), sem("s_norm")
            t_mm, t_done = sem("s_t_mm"), sem("s_t_copied")
            pv_mm, ot_hi_done, ot_done = sem("s_pv_mm"), sem("s_ot_hi"), sem("s_ot_split")
            y_mm, y_added = sem("s_y_mm"), sem("s_y_added")

            LAG_S, LAG_EXP, LAG_NORM, LAG_T, LAG_PV = 1, 2, 3, 4, 5

            def run_groups(eng, group):
                for g in range(2):
                    group(g, g, first=(g == 0), look=True, look2=True)
                with eng.Fori(1, GROUPS // 2 - 1) as i:
                    for x in range(2):
                        group(2 * i + x, x, first=False, look=True, look2=True)
                for x in range(2):
                    group(GROUPS - 2 + x, x, first=False, look=(x == 0))
                group(GROUPS, 0, first=False, look=False, drain=True)

            block = ph.enter_context(nc.Block())

            @block.sync
            def _(sp):
                for n in range(O_SPLIT):
                    weights.load(sp, n)
                sp.dma_start(r_raw[:], router.rearrange("(c p) e -> p c e", p=P)).then_inc(s_router, DMA)
                dram = xn_dram.rearrange("(t p) d -> p t d", p=P)
                with sp.Fori(0, GROUPS) as g:
                    sp.wait_ge(ln_f["s_xn"], 2 * g + 2)
                    sp.dma_start(dram[:, bass.ds(2 * g, 2), :], xn_sb[:, bass.ds(2 * g, 2), :]).then_inc(s_xn_stored, DMA)

            @block.gpsimd
            def _(pool):
                nc.gpsimd.memset(f32(kbd_hi[:]), 0.0).then_inc(s_zero, 1)
                nc.gpsimd.memset(f32(kbd_lo[:]), 0.0).then_inc(s_zero, 1)
                nc.gpsimd.memset(f32(r_hi[:]), 0.0).then_inc(s_rz, 1)
                nc.gpsimd.memset(f32(r_lo[:]), 0.0).then_inc(s_rz, 1)

                def group(g, x, first, look, look2=False, drain=False):
                    for p in range(PAIRS):
                        n = PAIRS * g + p
                        if p == 7 and look2:
                            ln_rstd(pool, ln, g + 2)
                        if (not first if p < LAG_NORM else not drain):
                            pool.wait_ge(rinv_done, n - 2)
                            prob = p_sb[:, (p - 3) % 4, :].rearrange("p (k j) -> p k j", k=4)
                            inv = rinv[:, (p - 3) % 4, :].unsqueeze(2).to_broadcast([P, 4, P])
                            nc.gpsimd.tensor_tensor(prob, prob, inv, ALU.mult).then_inc(norm_done, 1)
                        if p == 7 and not first:
                            ln_rstd(pool, ln_f, g - 1)

                for g in range(2):
                    ln_rstd(pool, ln, g)
                run_groups(pool, group)

            @block.tensor
            def _(pe):
                def turn_x(g):
                    pe.wait_ge(ln["s_xn"], 2 * g + 2)
                    wait(pe, v_done, 4 * g - 2)
                    for d in range(DC):
                        for u in range(2):
                            mm = pe.transpose(v_ps[:, (2 * d + u) * P:(2 * d + u + 1) * P],
                                              ln["xn"][:, u, d * P:(d + 1) * P], ident[:])
                    mm.then_inc(xt_mm, 1)

                def group(g, x, first, look, look2=False, drain=False):
                    for p in range(PAIRS):
                        n = PAIRS * g + p
                        cur, w = not drain, p % 2
                        if cur:
                            if p == 0:
                                if first:
                                    weights.wait_split(pe, K_SPLIT)
                                pe.wait_ge(xt_done, g + 1)
                            wait(pe, qk_done, n - 1)
                            for i, (hi, lo) in enumerate(((wq_hi, wq_lo), (wk_hi, wk_lo))):
                                mm = three_pass(pe, qk_ps[w][:, i * 2 * P:(i + 1) * 2 * P], [
                                    o for d in range(DC) for o in hi_lo(
                                        hi[:, d * E + p * P:d * E + (p + 1) * P], lo[:, d * E + p * P:d * E + (p + 1) * P],
                                        xt_hi[:, x, d, :], xt_lo[:, x, d, :])])
                            mm.then_inc(qk_mm, 1)
                        if (not first if p < LAG_S else cur):
                            wait(pe, qk_done, n)
                            wait(pe, sm_done, n - 2)
                            for u in range(2):
                                keys = lambda kbd: kbd[:, 1 - w, u, :, :].rearrange("p h j -> p (h j)")
                                rows = slice(u * P, (u + 1) * P)
                                mm = three_pass(pe, s_ps[1 - w][:, u * 2 * P:(u + 1) * 2 * P], hi_lo(
                                    qt_hi[:, 1 - w, rows], qt_lo[:, 1 - w, rows], keys(kbd_hi), keys(kbd_lo)))
                            mm.then_inc(s_mm, 1)
                        if p == 3 and look:
                            turn_x(g + 1)
                        if (not first if p < LAG_T else cur):
                            pe.wait_ge(norm_done, n - 3)
                            wait(pe, t_done, n - 4)
                            for k in range(4):
                                mm = pe.transpose(t_ps[:, k * P:(k + 1) * P],
                                                  p_sb[:, (p - 4) % 4, k * P:(k + 1) * P], ident[:])
                            mm.then_inc(t_mm, 1)
                        if (not first if p < LAG_PV else cur):
                            q, w2 = (p - 5) % PAIRS, 1 - w
                            pe.wait_ge(t_done, n - 4)
                            if p or not first:
                                wait(pe, v_done, 4 * g + (2 if p >= LAG_PV else -2 if p == 0 else 0))
                            if w2 == 0:
                                wait(pe, ot_done, PAIRS // 2 * g + (p - 5) // 2)
                            for u in range(2):
                                for h in range(2):
                                    k = 2 * u + h
                                    mm = pe.matmul(o_ps[h * HEAD:(h + 1) * HEAD, (2 * w2 + u) * P:(2 * w2 + u + 1) * P],
                                                   v_sb[:, u, q * P + h * HEAD:q * P + (h + 1) * HEAD],
                                                   pt_sb[:, w2, k * P:(k + 1) * P], start=True, stop=True)
                            mm.then_inc(pv_mm, 1)
                        if cur and w == 0:
                            half, u = p // 4, p // 2 % 2
                            rows = slice(u * P, (u + 1) * P)
                            wait(pe, v_done, 4 * g + p // 2)
                            if p == 0 and first:
                                weights.wait_split(pe, V_SPLIT)
                            if p == 4 and look:
                                pe.wait_ge(xt_done, g + 2)
                            three_pass(pe, v_ps[:], [
                                o for d in range(DC) for o in hi_lo(
                                    xt_hi[:, x, d, rows], xt_lo[:, x, d, rows],
                                    wv_hi[:, d * E + half * HALF:d * E + (half + 1) * HALF],
                                    wv_lo[:, d * E + half * HALF:d * E + (half + 1) * HALF])]).then_inc(v_mm, 1)
                        if w == 1 and (cur if p > LAG_PV + 1 else not first):
                            r = (p - 7) % PAIRS // 2
                            if first:
                                weights.wait_split(pe, O_SPLIT)
                            pe.wait_ge(ot_done, PAIRS // 2 * g + (p - 7) // 2 + 1)
                            if r == 0:
                                wait(pe, y_added, g)
                            for u in range(2):
                                tok = slice(u * P, (u + 1) * P)
                                for q in (2 * r, 2 * r + 1):
                                    c = slice(q * D, (q + 1) * D)
                                    for k, (a, m) in enumerate(hi_lo(ot_hi[:, q, tok], ot_lo[:, q, tok], wo_hi[:, c], wo_lo[:, c])):
                                        mm = pe.matmul(y_ps[:, u * D:(u + 1) * D], a, m, start=(q == 0 and u == 0 and k == 0),
                                                       stop=(q == PAIRS - 1 and k == 2), skip_group_check=True)
                            if r == 3:
                                mm.then_inc(y_mm, 1)

                turn_x(0)
                run_groups(pe, group)

            def k_part(kbd, w, h):
                r = slice(h * HEAD, (h + 1) * HEAD)
                return (qk_ps[w][r, 2 * P:4 * P].rearrange("p (u j) -> p u j", u=2), kbd[r, w, :, h, :])

            @block.scalar
            def _(act):
                def xt_hi_copy(g, x):
                    act.wait_ge(xt_mm, g + 1)
                    wait(act, v_mm, 4 * (g - 1))
                    split_hi_act(nc, xt_hi[:, x].rearrange("p d t -> p (d t)"), v_ps[:]).then_inc(xt_hi_done, 1)

                def group(g, x, first, look, look2=False, drain=False):
                    for p in range(PAIRS):
                        n = PAIRS * g + p
                        cur, w = not drain, p % 2
                        if cur:
                            act.wait_ge(qk_mm, n + 1)
                            wait(act, s_mm, n - 1)
                            split_hi_act(nc, qt_hi[:, w, :], qk_ps[w][:, 0:2 * P], SCALE).then_inc(qk_hi_done, 1)
                            for h in range(2):
                                src, dst = k_part(kbd_hi, w, h)
                                split_hi_act(nc, dst, src).then_inc(qk_hi_done, 1)
                        if (not first if p < LAG_EXP else cur):
                            act.wait_ge(max_done, n - 1)
                            wait(act, t_mm, n - 5)
                            s = (p - 2) % 4
                            if first and p == 2:
                                weights.wait_split(act, Q_SPLIT)
                            for k in range(4):
                                ex = nc.scalar.activation(p_sb[:, s, k * P:(k + 1) * P], sm_sb[:, w, k * P:(k + 1) * P],
                                                          ACT.Exp, bias=nmax[:, s, k:k + 1], scale=1.0,
                                                          accum_out=rsum[:, s, k:k + 1])
                            ex.then_inc(exp_done, 1)
                        if first and p == 3:
                            for i in range(2):
                                weights.split_hi(act, V_SPLIT + i)
                            act.wait_ge(s_router, DMA)
                            act.wait_ge(s_rz, 2)
                            nc.scalar.copy(r_hi[:, :, 0:EXPERTS], r_raw[:]).then_inc(s_rh, 1)
                        if p == 3 and look:
                            xt_hi_copy(g + 1, 1 - x)
                        if cur and w == 0:
                            act.wait_ge(v_mm, 4 * g + p // 2 + 1)
                            wait(act, pv_mm, PAIRS * g - (4 if p < 4 else 0))
                            if first and p == 0:
                                weights.wait_split(act, V_SPLIT)
                            nc.scalar.copy(v_sb[:, p // 2 % 2, p // 4 * HALF:(p // 4 + 1) * HALF], v_ps[:]).then_inc(v_done, 1)
                        if w == 0 and (not first if p < LAG_PV else cur):
                            q = (p - 5) % PAIRS
                            act.wait_ge(pv_mm, n - 4)
                            if p >= LAG_PV:
                                wait(act, y_mm, g)
                            split_hi_act(nc, ot_hi[:, q - 1:q + 1, :].rearrange("p a t -> p (a t)"),
                                         o_ps[:]).then_inc(ot_hi_done, 1)

                xt_hi_copy(0, 0)
                for n in range(V_SPLIT):
                    weights.split_hi(act, n)
                act.wait_ge(s_zero, 2)
                run_groups(act, group)

            @block.vector
            def _(dve):
                def xt_lo_copy(g, x):
                    dve.wait_ge(xt_hi_done, g + 1)
                    split_lo_dve(nc, xt_lo[:, x].rearrange("p d t -> p (d t)"), v_ps[:],
                                 xt_hi[:, x].rearrange("p d t -> p (d t)")).then_inc(xt_done, 1)

                def group(g, x, first, look, look2=False, drain=False):
                    for p in range(PAIRS):
                        n = PAIRS * g + p
                        cur, w = not drain, p % 2
                        if cur:
                            dve.wait_ge(qk_hi_done, 3 * n + 3)
                            split_lo_dve(nc, qt_lo[:, w, :], qk_ps[w][:, 0:2 * P], qt_hi[:, w, :], SCALE)
                            for h in range(2):
                                src, dst = k_part(kbd_lo, w, h)
                                lo = split_lo_dve(nc, dst, src, k_part(kbd_hi, w, h)[1])
                            lo.then_inc(qk_done, 1)
                        if (not first if p < LAG_NORM else cur):
                            dve.wait_ge(exp_done, n - 2)
                            nc.vector.reciprocal(rinv[:, (p - 3) % 4, :], rsum[:, (p - 3) % 4, :]).then_inc(rinv_done, 1)
                        if (not first if p < LAG_T else cur):
                            dve.wait_ge(t_mm, n - 3)
                            wait(dve, pv_mm, n - 5)
                            nc.vector.tensor_copy(pt_sb[:, w, :], t_ps[:]).then_inc(t_done, 1)
                        if (not first if p < LAG_S else cur):
                            dve.wait_ge(s_mm, n)
                            wait(dve, exp_done, n - 2)
                            nc.vector.tensor_tensor(sm_sb[:, 1 - w, :], s_ps[1 - w][:],
                                                    mask[:].rearrange("p k j -> p (k j)"), ALU.add).then_inc(sm_done, 1)
                            dve.wait_ge(sm_done, n)
                            nc.vector.tensor_reduce(nmax[:, (p - 1) % 4, :], sm_sb[:, 1 - w, :].rearrange("p (k j) -> p k j", k=4),
                                                    AX_X, ALU.max, negate=True).then_inc(max_done, 1)
                        if first and p == 3:
                            for i in range(2):
                                weights.split_lo(dve, V_SPLIT + i)
                            dve.wait_ge(s_rh, 1)
                            nc.vector.tensor_tensor(r_lo[:, :, 0:EXPERTS], r_raw[:], f32(r_hi[:, :, 0:EXPERTS]),
                                                    ALU.subtract).then_inc(s_rl, 1)
                        if p == 3 and look:
                            xt_lo_copy(g + 1, 1 - x)
                        if w == 0 and (not first if p < LAG_PV else cur):
                            q = (p - 5) % PAIRS
                            dve.wait_ge(ot_hi_done, PAIRS // 2 * g + (p - 4) // 2)
                            split_lo_dve(nc, ot_lo[:, q - 1:q + 1, :].rearrange("p a t -> p (a t)"), o_ps[:],
                                         ot_hi[:, q - 1:q + 1, :].rearrange("p a t -> p (a t)")).then_inc(ot_done, 1)
                        if p == 6 and not first:
                            dve.wait_ge(y_mm, g)
                            tiles = x_sb[:, bass.ds(2 * g - 2, 2), :].rearrange("p u d -> p (u d)")
                            nc.vector.tensor_tensor(tiles, y_ps[:], tiles, ALU.add).then_inc(y_added, 1)
                        if p == 7 and not first:
                            dve.wait_ge(y_added, g)
                            ln_stats(dve, ln_f, g - 1)
                        if p == 1 and not (isinstance(g, int) and g < 2):
                            ln_apply(dve, ln_f, g - 2, xn_sb)
                        if p == 0 and look:
                            ln_apply(dve, ln, g + 1)
                        if p == 5 and look2:
                            wait(dve, xt_mm, g + 2)
                            ln_stats(dve, ln, g + 2)

                ln_stats(dve, ln, 0)
                ln_apply(dve, ln, 0)
                xt_lo_copy(0, 0)
                ln_stats(dve, ln, 1)
                for n in range(V_SPLIT):
                    weights.split_lo(dve, n)
                run_groups(dve, group)
                ln_apply(dve, ln_f, GROUPS - 1, xn_sb)

        moe(nc, sem, sbuf, psum, x_sb, xn_sb, xn_dram, s_xn_stored, ident, r_hi, r_lo, w_gate, w_up, w_down, slots,
            s_fill, FILLS, out)


def moe(nc, sem, sbuf, psum, x_sb, xn_sb, xn_dram, s_xn_stored, ident, r_hi, r_lo, w_gate, w_up, w_down, slots,
        s_fill, fills, out):
    _, TILES, D = x_sb.shape
    DC = D // P
    GROUPS = TILES // 2
    EXPERTS, _, F = w_gate.shape
    FC = F // P
    GU = DC * F
    TE = TILES * EXPERTS
    SLOT_TILES = slots.shape[0] // P
    MAX_TILES = SLOT_TILES - 1
    COLS = 2 * GU + FC * D
    PIECES = 3
    CUT = COLS // PIECES
    MIDDLE = TILES * P // 2
    F16 = mybir.dt.float16
    assert MIDDLE <= 2048 and P - 1 <= 2048 and SLOT_TILES <= 2048 and COLS == CUT * PIECES and MIN_TILES > PIECES + 1

    with ExitStack() as ph:
        gate = [sbuf(ph, f"gate{k}", [P, TILES]) for k in range(2)]
        slot = [sbuf(ph, f"slot{k}", [P, TILES], mybir.dt.uint32) for k in range(2)]
        first_tile = sbuf(ph, "first_tile", [P, EXPERTS + 1], mybir.dt.int32)
        last_tile = sbuf(ph, "last_tile", [P, EXPERTS], mybir.dt.int32)
        pairs = sbuf(ph, "pairs", [P, 1], mybir.dt.int32)
        token_of = sbuf(ph, "token_of", [P, SLOT_TILES + 1], mybir.dt.uint32)
        raw = sbuf(ph, "e_raw", [P, COLS])
        w_hi = sbuf(ph, "e_w_hi", [P, 2, COLS], F32R)
        w_lo = sbuf(ph, "e_w_lo", [P, 2, COLS], F32R)
        zero = sbuf(ph, "e_zero", [P, 1])
        s_raw, s_zero, s_whi, s_wlo = sem("e_raw_loaded"), sem("e_zero_set"), sem("e_w_hi_done"), sem("e_w_split")

        def load_expert(sp, e):
            sp.dma_start(raw[:, 0:GU].rearrange("p (c f) -> p c f", c=DC),
                         w_gate[e].rearrange("(c p) f -> p c f", p=P)).then_inc(s_raw, DMA)
            sp.dma_start(raw[:, GU:2 * GU].rearrange("p (c f) -> p c f", c=DC),
                         w_up[e].rearrange("(c p) f -> p c f", p=P)).then_inc(s_raw, DMA)
            sp.dma_start(raw[:, 2 * GU:].rearrange("p (c d) -> p c d", c=FC),
                         w_down[e].rearrange("(c p) d -> p c d", p=P)).then_inc(s_raw, DMA)

        with ExitStack() as rt:
            xt_hi = sbuf(rt, "f_xt_hi", [P, 2, DC, 2 * P], F32R)
            xt_lo = sbuf(rt, "f_xt_lo", [P, 2, DC, 2 * P], F32R)
            lt_sb = sbuf(rt, "lt_sb", [P, 2, 2 * P])
            logit = sbuf(rt, "logit", [P, TILES, EXPERTS])
            prob = sbuf(rt, "prob", [P, TILES, EXPERTS])
            tmp = sbuf(rt, "r_tmp", [P, TILES, EXPERTS])
            hot = [sbuf(rt, f"hot{i}", [P, TILES, EXPERTS]) for i in range(2)]
            both = sbuf(rt, "hot_both", [P, TILES, EXPERTS])
            place = sbuf(rt, "place", [P, TILES, EXPERTS])
            rank = sbuf(rt, "rank", [P, TILES, EXPERTS])
            col = [sbuf(rt, f"r_col{i}", [P, TILES]) for i in range(5)]
            before = sbuf(rt, "before", [P, P])
            ones = sbuf(rt, "ones", [P, P])
            seen = sbuf(rt, "seen", [P, EXPERTS, TILES])
            cnt = sbuf(rt, "cnt", [P, EXPERTS])
            cnt_int = sbuf(rt, "cnt_int", [P, EXPERTS], mybir.dt.int32)
            tiles_int = sbuf(rt, "tiles_int", [P, EXPERTS], mybir.dt.int32)
            tiles = sbuf(rt, "tiles_of", [P, EXPERTS])
            upto = sbuf(rt, "tiles_upto", [P, EXPERTS + 1])
            HOTS = 8
            column = sbuf(rt, "column", [P, P], F16)
            number = sbuf(rt, "number", [P, TILES])
            of_slot = sbuf(rt, "of_slot", [P, 2, TILES])
            slot_int = sbuf(rt, "slot_int", [P, 2, TILES], mybir.dt.int32)
            slot_tile_int = sbuf(rt, "slot_tile_int", [P, 2, TILES], mybir.dt.int32)
            slot_tile = sbuf(rt, "slot_tile", [P, 2, TILES])
            slot_row = sbuf(rt, "slot_row", [P, 2, TILES])
            token_f = sbuf(rt, "token_f", [P, SLOT_TILES])
            hot_row = sbuf(rt, "hot_row", [P, HOTS, P], F16)
            hot_tile = sbuf(rt, "hot_tile", [P, HOTS, SLOT_TILES], F16)

            xt_ps = [psum(rt, f"fxt_ps{i}") for i in range(2)]
            lt_ps = [psum(rt, f"flt_ps{i}") for i in range(2)]
            lg_ps = [psum(rt, f"flg_ps{i}") for i in range(2)]
            both_ps = psum(rt, "f_both_ps")
            pre_ps, tot_ps = both_ps[:, 0:TE], both_ps[:, TE:2 * TE]
            token_ps = psum(rt, "f_token_ps")
            s_const = sem("f_const")
            xt_mm, xt_h, xt_l = sem("f_xt_mm"), sem("f_xt_hi_done"), sem("f_xt_split")
            lt_mm, lt_done, lg_mm, lg_done = sem("f_lt_mm"), sem("f_lt_copied"), sem("f_lg_mm"), sem("f_lg_copied")
            chain, s_exp, s_count = sem("f_chain"), sem("f_exp"), sem("f_count_mm")
            hot_done, hot_used = sem("f_onehot_done"), sem("f_onehot_mm")
            LOGIT_MINUS_MAX, SECOND_MINUS_FIRST, ASSIGNED = 2, 16, 18

            block = rt.enter_context(nc.Block())

            @block.sync
            def _(sp):
                load_expert(sp, 0)

            @block.gpsimd
            def _(pool):
                nc.gpsimd.memset(zero[:], 0.0).then_inc(s_zero, 1)
                for e in range(EXPERTS):
                    nc.gpsimd.memset(rank[:, :, e:e + 1], float(EXPERTS - e)).then_inc(s_const, 1)
                nc.gpsimd.memset(ones[:], 1.0).then_inc(s_const, 1)
                nc.gpsimd.iota(column[:], pattern=[[1, P]], base=0, channel_multiplier=0,
                               allow_small_or_imprecise_dtypes=True).then_inc(s_const, 1)
                nc.gpsimd.iota(number[:], pattern=[[P, TILES]], base=-MIDDLE, channel_multiplier=1,
                               allow_small_or_imprecise_dtypes=True).then_inc(s_const, 1)
                pool.wait_ge(s_const, EXPERTS + 3)
                nc.gpsimd.affine_select(out=before[:], in_=ones[:], compare_op=ALU.is_gt, fill=0.0, base=0,
                                        pattern=[[1, P]], channel_multiplier=-1).then_inc(s_const, 1)
                pool.wait_ge(s_raw, 3 * DMA)
                pool.wait_ge(s_zero, 1)
                for c in range(PIECES):
                    cut = slice(c * CUT, (c + 1) * CUT)
                    round_pool(nc, w_hi[:, 0, cut], raw[:, cut], zero).then_inc(s_whi, 1)
                    pool.wait_ge(s_whi, c + 1)
                    nc.gpsimd.tensor_tensor(w_lo[:, 0, cut], raw[:, cut], f32(w_hi[:, 0, cut]), ALU.subtract).then_inc(s_wlo, 1)
                pool.wait_ge(s_xn_stored, GROUPS * DMA)
                pool.wait_ge(s_fill, fills * DMA)

            @block.tensor
            def _(pe):
                def turn_x(g):
                    wait(pe, xt_l, g - 1)
                    for d in range(DC):
                        for u in range(2):
                            mm = pe.transpose(xt_ps[g % 2][:, (2 * d + u) * P:(2 * d + u + 1) * P],
                                              xn_sb[:, 2 * g + u, d * P:(d + 1) * P], ident[:])
                    mm.then_inc(xt_mm, 1)

                def logits(g):
                    pe.wait_ge(xt_l, g + 1)
                    wait(pe, lt_done, g - 1)
                    w = g % 2
                    three_pass(pe, lt_ps[w][:, 0:2 * P], [
                        x for d in range(DC) for x in hi_lo(r_hi[:, d, :], r_lo[:, d, :],
                                                            xt_hi[:, w, d, :], xt_lo[:, w, d, :])]).then_inc(lt_mm, 1)

                def turn_logits(g):
                    pe.wait_ge(lt_done, g + 1)
                    wait(pe, lg_done, g - 1)
                    for u in range(2):
                        mm = pe.transpose(lg_ps[g % 2][:, u * P:(u + 1) * P], lt_sb[:, g % 2, u * P:(u + 1) * P], ident[:])
                    mm.then_inc(lg_mm, 1)

                for i in range(GROUPS + 2):
                    if i < GROUPS:
                        turn_x(i)
                    if i >= 2:
                        turn_logits(i - 2)
                    if 1 <= i < GROUPS + 1:
                        logits(i - 1)
                pe.wait_ge(s_const, EXPERTS + 4)
                pe.wait_ge(chain, ASSIGNED)
                flat = both[:].rearrange("p t e -> p (t e)")
                pe.matmul(pre_ps[:, 0:TE], before[:], flat, start=True, stop=True)
                pe.matmul(tot_ps[:, 0:TE], ones[:], flat, start=True, stop=True).then_inc(s_count, 1)
                for n in range(2 * TILES):
                    pe.wait_ge(hot_done, 2 * n + 2)
                    pe.matmul(token_ps[:, 0:SLOT_TILES], hot_row[:, n % HOTS, :], hot_tile[:, n % HOTS, :],
                              start=(n == 0), stop=(n == 2 * TILES - 1)).then_inc(hot_used, 1)

            @block.scalar
            def _(act):
                for i in range(GROUPS + 1):
                    if i < GROUPS:
                        act.wait_ge(xt_mm, i + 1)
                        wait(act, lt_mm, i - 1)
                        split_hi_act(nc, xt_hi[:, i % 2].rearrange("p d t -> p (d t)"), xt_ps[i % 2][:]).then_inc(xt_h, 1)
                    if i:
                        g = i - 1
                        act.wait_ge(lt_mm, g + 1)
                        wait(act, lg_mm, g - 1)
                        nc.scalar.copy(lt_sb[:, g % 2, :], lt_ps[g % 2][:, 0:2 * P]).then_inc(lt_done, 1)
                act.wait_ge(chain, LOGIT_MINUS_MAX)
                nc.scalar.activation(prob[:], tmp[:], ACT.Exp).then_inc(s_exp, 1)
                act.wait_ge(chain, SECOND_MINUS_FIRST)
                nc.scalar.activation(col[4][:], col[3][:], ACT.Exp).then_inc(s_exp, 1)

            @block.vector
            def _(dve):
                V = nc.vector
                for i in range(GROUPS + 3):
                    if 1 <= i < GROUPS + 1:
                        g = i - 1
                        dve.wait_ge(xt_h, g + 1)
                        split_lo_dve(nc, xt_lo[:, g % 2].rearrange("p d t -> p (d t)"), xt_ps[g % 2][:],
                                     xt_hi[:, g % 2].rearrange("p d t -> p (d t)")).then_inc(xt_l, 1)
                    if i >= 3:
                        g = i - 3
                        dve.wait_ge(lg_mm, g + 1)
                        V.tensor_copy(logit[:, 2 * g:2 * g + 2, :],
                                      lg_ps[g % 2][:, 0:2 * P].rearrange("p (u e) -> p u e", u=2)[:, :, 0:EXPERTS]).then_inc(lg_done, 1)

                count = [0]

                def link(ins):
                    count[0] += 1
                    ins.then_inc(chain, 1)
                    dve.wait_ge(chain, count[0])

                def wide(c):
                    return c[:].unsqueeze(2).to_broadcast([P, TILES, EXPERTS])

                dve.wait_ge(lg_done, GROUPS)
                dve.wait_ge(s_const, EXPERTS + 1)
                link(V.tensor_reduce(col[0][:], logit[:], AX_X, ALU.max))
                link(V.tensor_tensor(tmp[:], logit[:], wide(col[0]), ALU.subtract))
                assert count[0] == LOGIT_MINUS_MAX
                dve.wait_ge(s_exp, 1)
                link(V.tensor_reduce(col[0][:], prob[:], AX_X, ALU.add))
                link(V.reciprocal(col[1][:], col[0][:]))
                link(V.tensor_tensor(prob[:], prob[:], wide(col[1]), ALU.mult))
                for k in range(2):
                    link(V.tensor_reduce(col[1 + k][:], prob[:], AX_X, ALU.max))
                    link(V.tensor_tensor(tmp[:], prob[:], wide(col[1 + k]), ALU.is_equal))
                    link(V.tensor_tensor(tmp[:], tmp[:], rank[:], ALU.mult))
                    link(V.tensor_reduce(col[0][:], tmp[:], AX_X, ALU.max))
                    if k == 0:
                        link(V.tensor_tensor(hot[0][:], tmp[:], wide(col[0]), ALU.is_equal))
                        link(V.scalar_tensor_tensor(out=prob[:].rearrange("p t e -> p (t e)"),
                                                    in0=hot[0][:].rearrange("p t e -> p (t e)"), scalar=-2.0,
                                                    in1=prob[:].rearrange("p t e -> p (t e)"), op0=ALU.mult, op1=ALU.add))
                link(V.tensor_tensor(col[3][:], col[2][:], col[1][:], ALU.subtract))
                assert count[0] == SECOND_MINUS_FIRST
                link(V.tensor_tensor(hot[1][:], tmp[:], wide(col[0]), ALU.is_equal))
                link(V.tensor_tensor(both[:], hot[0][:], hot[1][:], ALU.add))
                assert count[0] == ASSIGNED
                dve.wait_ge(s_exp, 2)
                link(V.tensor_scalar(col[0][:], col[4][:], 1.0, None, ALU.add))
                link(V.reciprocal(gate[0][:], col[0][:]))
                link(V.tensor_tensor(gate[1][:], col[4][:], gate[0][:], ALU.mult))
                dve.wait_ge(s_count, 1)
                link(V.tensor_copy(tmp[:].rearrange("p t e -> p (t e)"), tot_ps[:, 0:TE]))
                for e in range(EXPERTS):
                    last = V.tensor_tensor_scan(seen[:, e, :], ones[:, 0:TILES], tmp[:, :, e], 0.0, ALU.mult, ALU.add)
                link(last)
                link(V.tensor_scalar(cnt_int[:], seen[:, :, TILES - 1], float(P - 1), None, ALU.add))
                link(V.tensor_scalar(tiles_int[:], cnt_int[:], P.bit_length() - 1, None, ALU.arith_shift_right))
                link(V.tensor_scalar(tiles[:], tiles_int[:], float(MIN_TILES), None, ALU.max))
                link(V.memset(upto[:, 0:1], 0.0))
                link(V.tensor_tensor_scan(upto[:, 1:EXPERTS + 1], ones[:, 0:EXPERTS], tiles[:], 0.0, ALU.mult, ALU.add))
                link(V.tensor_copy(first_tile[:], upto[:]))
                link(V.tensor_scalar(pairs[:], first_tile[:, EXPERTS:EXPERTS + 1], 1, None, ALU.arith_shift_right))
                link(V.tensor_scalar(last_tile[:], upto[:, 1:EXPERTS + 1], -1.0, None, ALU.add))
                link(V.tensor_scalar(cnt[:], upto[:, 0:EXPERTS], float(P), None, ALU.mult))
                link(V.tensor_tensor(place[:].rearrange("p t e -> p (t e)"), pre_ps[:, 0:TE],
                                     tmp[:].rearrange("p t e -> p (t e)"), ALU.subtract))
                link(V.tensor_tensor(place[:], place[:], seen[:].rearrange("p e t -> p t e"), ALU.add))
                link(V.tensor_tensor(place[:], place[:], cnt[:].unsqueeze(1).to_broadcast([P, TILES, EXPERTS]), ALU.add))
                for k in range(2):
                    link(V.tensor_tensor(hot[k][:], hot[k][:], place[:], ALU.mult))
                    link(V.tensor_reduce(of_slot[:, k, :], hot[k][:], AX_X, ALU.add))
                    V.tensor_copy(slot[k][:], of_slot[:, k, :]).then_inc(chain, 1)
                    count[0] += 1
                link(V.tensor_copy(slot_int[:], of_slot[:]))
                link(V.tensor_scalar(slot_tile_int[:], slot_int[:], P.bit_length() - 1, None, ALU.arith_shift_right))
                link(V.tensor_scalar(slot_tile[:], slot_tile_int[:], 0.0, None, ALU.max))
                link(V.scalar_tensor_tensor(out=slot_row[:], in0=slot_tile[:], scalar=-float(P), in1=of_slot[:],
                                            op0=ALU.mult, op1=ALU.add))
                dve.wait_ge(s_const, EXPERTS + 3)
                for n in range(2 * TILES):
                    t, k = n // 2, n % 2
                    wait(dve, hot_used, n - HOTS + 1)
                    V.tensor_scalar(hot_row[:, n % HOTS, :], column[:], slot_row[:, k, t:t + 1], None,
                                    ALU.is_equal).then_inc(hot_done, 1)
                    V.tensor_scalar(hot_tile[:, n % HOTS, :], column[:, 0:SLOT_TILES], slot_tile[:, k, t:t + 1],
                                    number[:, t:t + 1], ALU.is_equal, ALU.mult).then_inc(hot_done, 1)
                dve.wait_ge(hot_used, 2 * TILES)
                link(V.memset(token_of[:, SLOT_TILES:SLOT_TILES + 1], 0))
                link(V.tensor_scalar(token_f[:], token_ps[:, 0:SLOT_TILES], float(MIDDLE), None, ALU.add))
                link(V.tensor_copy(token_of[:, 0:SLOT_TILES], token_f[:]))

        with ExitStack() as ex:
            token_now = [sbuf(ex, f"e_token_now{i}", [P, 1], mybir.dt.uint32) for i in range(2)]
            warm = sbuf(ex, "e_warm", [P, 1])
            s_warm = sem("e_silu_table")
            none = sbuf(ex, "e_none", [P, 1], mybir.dt.uint32)
            dummy = [sbuf(ex, f"e_dummy{i}", [P, 1]) for i in range(2)]
            xs_in = [sbuf(ex, f"e_xs_in{i}", [P, D]) for i in range(2)]
            xs_sb = sbuf(ex, "e_xs", [P, D])
            xt_hi = sbuf(ex, "e_xt_hi", [P, D], F32R)
            xt_lo = sbuf(ex, "e_xt_lo", [P, D], F32R)
            silu_sb = sbuf(ex, "e_silu", [P, F])
            h_sb = sbuf(ex, "e_h", [P, F])
            ht_hi = sbuf(ex, "e_ht_hi", [P, F], F32R)
            ht_lo = sbuf(ex, "e_ht_lo", [P, F], F32R)
            ys_sb = sbuf(ex, "e_ys", [P, D])
            xt_ps = psum(ex, "e_xt_ps")
            g_ps = psum(ex, "e_g_ps")
            u_ps = psum(ex, "e_u_ps")
            ht_ps = psum(ex, "e_ht_ps")
            y_ps = psum(ex, "e_y_ps")
            s_now, s_moved, s_dummy = sem("e_token_now_set"), sem("e_xs_moved"), sem("e_dummy_done")
            s_xs, xt_mm, xt_h, xt_l = [sem(f"e_xs_loaded{i}") for i in range(2)], sem("e_xt_mm"), sem("e_xt_hi_done"), sem("e_xt_split")
            g_mm, u_mm, silu_done, h_done = sem("e_g_mm"), sem("e_u_mm"), sem("e_silu_done"), sem("e_h_done")
            ht_mm, ht_h, ht_l = sem("e_ht_mm"), sem("e_ht_hi_done"), sem("e_ht_split")
            y_mm, y_copied, s_stored = sem("e_y_mm"), sem("e_y_copied"), sem("e_ys_stored")
            s_ended = sem("e_transfers_ended")

            def tile_count(eng):
                return eng.value_load(first_tile[0:1, EXPERTS:EXPERTS + 1], min_val=MIN_TILES * EXPERTS, max_val=MAX_TILES)

            def last_of(eng, e):
                return eng.value_load(last_tile[0:1, e:e + 1], min_val=MIN_TILES * (e + 1) - 1,
                                      max_val=MAX_TILES - MIN_TILES * (EXPERTS - 1 - e) - 1)

            def rows(i):
                return bass.ds(i * P, P)

            def run_tiles(eng, tile):
                start = 0
                for e in range(EXPERTS):
                    bound = dict(min_val=MIN_TILES * (e + 1), max_val=MAX_TILES - MIN_TILES * (EXPERTS - 1 - e))
                    end = eng.value_load(first_tile[0:1, e + 1:e + 2], **bound)
                    if e:
                        tile(start, last, e, None)
                    for piece in range(PIECES):
                        tile(start + (piece + 1), start + piece if piece else start, e, piece if e + 1 < EXPERTS else None)
                    with eng.Fori(start + (PIECES + 1), end) as i:
                        tile(i, i - 1, e, None)
                    start, last = end, last_of(eng, e)
                return last

            block = ex.enter_context(nc.Block())

            @block.sync
            def _(sp):
                for e in range(1, EXPERTS):
                    sp.wait_ge(s_wlo, PIECES * e)
                    load_expert(sp, e)
                sp.wait_ge(s_raw, 3 * DMA * EXPERTS)

            @block.gpsimd
            def _(pool):
                def gather(i, half):
                    wait(pool, s_moved, i - 1 if isinstance(i, int) else i + -1)
                    nc.gpsimd.tensor_tensor(token_now[half][:], token_of[:, bass.ds(i, 1)], none[:], ALU.add).then_inc(s_now, 1)
                    pool.wait_ge(s_now, i + 1)
                    nc.gpsimd.tensor_tensor(dummy[half][:], zero[:], zero[:], ALU.add).then_inc(s_dummy, 1)
                    pool.indirect_dma_start(
                        out=xs_in[half][:], out_offset=None, in_=xn_dram,
                        in_offset=bass.IndirectOffsetOnAxis(ap=token_now[half][:], axis=0)).then_inc(s_xs[half], DMA)

                def move(i, pair, half):
                    pool.wait_ge(s_xs[half], DMA * pair + DMA)
                    wait(pool, s_dummy, i)
                    wait(pool, xt_mm, i)
                    nc.gpsimd.tensor_tensor(xs_sb[:], xs_in[half][:], zero[:].to_broadcast([P, D]), ALU.add).then_inc(s_moved, 1)

                more_pairs = pool.value_load(pairs[0:1, 0:1], min_val=MIN_TILES * EXPERTS // 2, max_val=MAX_TILES // 2)
                nc.gpsimd.memset(none[:], 0).then_inc(s_zero, 1)
                pool.wait_ge(s_zero, 2)
                for half in range(2):
                    gather(half, half)
                for half in range(2):
                    move(half, 0, half)
                    gather(2 + half, half)
                with pool.Fori(1, more_pairs) as j:
                    for half in range(2):
                        move(2 * j + half, j, half)
                        gather(2 * j + (2 + half), half)
                for half in range(2):
                    move(2 * more_pairs + half, more_pairs, half)

            @block.tensor
            def _(pe):
                def turn_x(i):
                    pe.wait_ge(s_moved, i + 1)
                    wait(pe, xt_l, i)
                    for d in range(DC):
                        mm = pe.transpose(xt_ps[:, d * P:(d + 1) * P], xs_sb[:, d * P:(d + 1) * P], ident[:])
                    mm.then_inc(xt_mm, 1)

                def turn_h(i):
                    wait(pe, h_done, i + 1)
                    wait(pe, ht_l, i)
                    for f in range(FC):
                        mm = pe.transpose(ht_ps[:, f * P:(f + 1) * P], h_sb[:, f * P:(f + 1) * P], ident[:])
                    mm.then_inc(ht_mm, 1)

                def gate_up(i, w):
                    pe.wait_ge(xt_l, i + 1)
                    for base, ps, s in ((0, g_ps, g_mm), (GU, u_ps, u_mm)):
                        three_pass(pe, ps[:], [x for d in range(DC) for x in hi_lo(
                            xt_hi[:, d * P:(d + 1) * P], xt_lo[:, d * P:(d + 1) * P],
                            w_hi[:, w, base + d * F:base + (d + 1) * F], w_lo[:, w, base + d * F:base + (d + 1) * F])]).then_inc(s, 1)

                def down(i, w):
                    pe.wait_ge(ht_l, i + 1)
                    wait(pe, y_copied, i)
                    three_pass(pe, y_ps[:, 0:D], [x for f in range(FC) for x in hi_lo(
                        ht_hi[:, f * P:(f + 1) * P], ht_lo[:, f * P:(f + 1) * P],
                        w_hi[:, w, 2 * GU + f * D:2 * GU + (f + 1) * D],
                        w_lo[:, w, 2 * GU + f * D:2 * GU + (f + 1) * D])]).then_inc(y_mm, 1)

                def step(i, before, w, w_before):
                    turn_x(i + 1)
                    turn_h(before)
                    gate_up(i, w)
                    down(before, w_before)

                turn_x(0)
                turn_x(1)
                gate_up(0, 0)
                for e in range(EXPERTS):
                    bound = dict(min_val=MIN_TILES * (e + 1), max_val=MAX_TILES - MIN_TILES * (EXPERTS - 1 - e))
                    if e:
                        pe.wait_ge(s_wlo, PIECES * (e + 1))
                        step(start, last, e % 2, 1 - e % 2)
                    end = pe.value_load(first_tile[0:1, e + 1:e + 2], **bound)
                    with pe.Fori(start + 1 if e else 1, end) as i:
                        step(i, i - 1, e % 2, e % 2)
                    start, last = end, last_of(pe, e)
                turn_h(last)
                down(last, (EXPERTS - 1) % 2)

            @block.scalar
            def _(act):
                def step(i):
                    act.wait_ge(xt_mm, i + 1)
                    wait(act, u_mm, i)
                    split_hi_act(nc, xt_hi[:], xt_ps[:, 0:D]).then_inc(xt_h, 1)

                def rest(i):
                    act.wait_ge(g_mm, i + 1)
                    wait(act, h_done, i)
                    nc.scalar.activation(silu_sb[:], g_ps[:], ACT.Silu).then_inc(silu_done, 1)

                def ht_hi_copy(i):
                    act.wait_ge(ht_mm, i + 1)
                    wait(act, y_mm, i)
                    split_hi_act(nc, ht_hi[:], ht_ps[:]).then_inc(ht_h, 1)

                def y_copy(i):
                    act.wait_ge(y_mm, i + 1)
                    wait(act, s_stored, DMA * i)
                    nc.scalar.copy(ys_sb[:], y_ps[:, 0:D]).then_inc(y_copied, 1)
                    act.wait_ge(y_copied, i + 1)
                    act.dma_start(slots[rows(i), :], ys_sb[:]).then_inc(s_stored, DMA)

                def tile(i, before, e, piece):
                    ht_hi_copy(before)
                    rest(i)
                    step(i + 1)
                    if piece is not None:
                        if piece == 0:
                            act.wait_ge(s_raw, 3 * DMA * (e + 2))
                        cut = slice(piece * CUT, (piece + 1) * CUT)
                        split_hi_act(nc, w_hi[:, (e + 1) % 2, cut], raw[:, cut]).then_inc(s_whi, 1)
                    y_copy(before)

                total = tile_count(act)
                nc.scalar.activation(warm[:], zero[:], ACT.Silu).then_inc(s_warm, 1)
                step(0)
                rest(0)
                step(1)
                last = run_tiles(act, tile)
                ht_hi_copy(last)
                y_copy(last)
                act.wait_ge(s_stored, DMA * total)
                act.sem_inc(s_ended, 1)

            @block.vector
            def _(dve):
                def xt_lo_copy(i):
                    dve.wait_ge(xt_h, i + 1)
                    split_lo_dve(nc, xt_lo[:], xt_ps[:, 0:D], xt_hi[:]).then_inc(xt_l, 1)

                def product(i):
                    dve.wait_ge(u_mm, i + 1)
                    dve.wait_ge(silu_done, i + 1)
                    wait(dve, ht_mm, i)
                    nc.vector.tensor_tensor(h_sb[:], u_ps[:], silu_sb[:], ALU.mult).then_inc(h_done, 1)

                def ht_lo_copy(i):
                    dve.wait_ge(ht_h, i + 1)
                    split_lo_dve(nc, ht_lo[:], ht_ps[:], ht_hi[:]).then_inc(ht_l, 1)

                def tile(i, before, e, piece):
                    ht_lo_copy(before)
                    product(i)
                    xt_lo_copy(i + 1)
                    if piece is not None:
                        dve.wait_ge(s_whi, PIECES * (e + 1) + piece + 1)
                        cut = slice(piece * CUT, (piece + 1) * CUT)
                        split_lo_dve(nc, w_lo[:, (e + 1) % 2, cut], raw[:, cut], w_hi[:, (e + 1) % 2, cut]).then_inc(s_wlo, 1)

                xt_lo_copy(0)
                product(0)
                xt_lo_copy(1)
                last = run_tiles(dve, tile)
                ht_lo_copy(last)

        BUFS = 8
        y_sb = sbuf(ph, "c_y", [P, BUFS, 2, D])
        s_y = [sem(f"c_gathered{i}") for i in range(BUFS)]
        s_half, s_sum, s_out = sem("c_first_added"), sem("c_added"), sem("out_stored")
        STORE = 4
        block = ph.enter_context(nc.Block())

        @block.gpsimd
        def _(pool):
            for t in range(TILES):
                wait(pool, s_sum, t - BUFS + 1)
                for k in range(2):
                    pool.indirect_dma_start(
                        out=y_sb[:, t % BUFS, k, :], out_offset=None, in_=slots,
                        in_offset=bass.IndirectOffsetOnAxis(ap=slot[k][:, t:t + 1], axis=0)).then_inc(s_y[t % BUFS], DMA)

        @block.vector
        def _(dve):
            def add(t, k):
                return nc.vector.scalar_tensor_tensor(
                    out=x_sb[:, t, :], in0=y_sb[:, t % BUFS, k, :], scalar=gate[k][:, t:t + 1], in1=x_sb[:, t, :],
                    op0=ALU.mult, op1=ALU.add)

            for t in range(TILES):
                dve.wait_ge(s_y[t % BUFS], 2 * DMA * (t // BUFS + 1))
                add(t, 0).then_inc(s_half, 1)
                dve.wait_ge(s_half, t + 1)
                add(t, 1).then_inc(s_sum, 1)

        @block.sync
        def _(sp):
            dram = out.rearrange("(t p) d -> p t d", p=P)
            for t in range(0, TILES, STORE):
                sp.wait_ge(s_sum, t + STORE)
                sp.dma_start(dram[:, t:t + STORE, :], x_sb[:, t:t + STORE, :]).then_inc(s_out, DMA)
            sp.wait_ge(s_out, TILES // STORE * DMA)


def kernel(**inputs):
    import numpy as np
    import concourse.bacc as bacc
    from concourse.bass_utils import run_bass_kernel_spmd

    a = {k: np.asarray(v) for k, v in inputs.items()}
    x = a["x"]
    B, S, D = x.shape
    _, J, C = a["ctx_768"].shape
    tiles = B * S // P
    arrays = {
        "x": x.reshape(B * S, D),
        "ctx_t": a["ctx_768"].reshape(tiles, 2 * J, C).transpose(0, 2, 1),
        "xattn_wq": a["L0_xattn_Wq"], "xattn_wk": a["L0_xattn_Wk"], "xattn_wv": a["L0_xattn_Wv"],
        "xattn_wo": a["L0_xattn_Wo"], "xattn_bo": a["L0_xattn_bo"],
        "attn_wq": a["L0_attn_wq"].T, "attn_wk": a["L0_attn_wk"].T, "attn_wv": a["L0_attn_wv"].T,
        "attn_wo": a["L0_attn_wo"].T,
        "router": a["L0_ffn_router_kernel_DE"], "gate": a["L0_ffn_kernel_gating_EDF"],
        "up": a["L0_ffn_kernel_up_EDF"], "down": a["L0_ffn_kernel_down_EFD"],
    }
    nc = bacc.Bacc("TRN2", target_bir_lowering=False, num_devices=1)
    feed, args = {}, []
    for name, arr in arrays.items():
        arr = np.ascontiguousarray(arr)
        feed["in_" + name] = arr
        args.append(nc.dram_tensor("in_" + name, arr.shape, mybir.dt.from_np(arr.dtype), kind="ExternalInput").ap())
    args.append(nc.dram_tensor("out_x", (B * S, D), F32, kind="ExternalOutput").ap())
    layer_kernel(nc, *args)
    r = run_bass_kernel_spmd(nc, [feed], core_ids=[0])
    return r.results[0]["out_x"].reshape(B, S, D)
```
